# Optimizing a Trainium2 kernel written in Bass

```python
import numpy as np
import jax
import jax.numpy as jnp

def _softmax(x, axis=-1):
    return jax.nn.softmax(x, axis=axis)

def _gelu(x):
    return jax.nn.gelu(x, approximate=True)

def _silu(x):
    return jax.nn.silu(x)

def _sigmoid(x):
    return jax.nn.sigmoid(x)

def _layernorm(x, axis=-1, eps=1e-05):
    m = jnp.mean(x, axis=axis, keepdims=True)
    v = jnp.var(x, axis=axis, keepdims=True)
    return (x - m) / jnp.sqrt(v + eps)

def _scatter_add(tgt, idx, src, axis=0):
    return tgt.at[idx].add(src)

def _segment_sum(src, seg, n):
    return jax.ops.segment_sum(src, seg, n)
kernel_name = 'mk_seq_postln_d1_jaxref_r4_7e9052'

def setup_inputs(seed: int=0):
    np.random.seed(seed)
    _w = jnp.asarray

    def _L0_attn_setup():
        import jax, jax.numpy as jnp
        import numpy as np
        B, S, D, H = (2, 512, 256, 16)
        DEPTH = D // H
        EPS = 1e-06

        def _split_heads(t):
            b, s, _ = t.shape
            return t.reshape(b, s, H, DEPTH).transpose(0, 2, 1, 3)
        key = jax.random.key(seed)
        ks = jax.random.split(key, 6)
        glorot = lambda k: jax.random.uniform(k, (D, D), jnp.float32, -1.0, 1.0) * np.sqrt(6.0 / (D + D))
        return {'x': jax.random.normal(ks[0], (B, S, D), jnp.float32), 'Wq': glorot(ks[1]), 'bq': jnp.zeros((D,), jnp.float32), 'Wk': glorot(ks[2]), 'bk': jnp.zeros((D,), jnp.float32), 'Wv': glorot(ks[3]), 'bv': jnp.zeros((D,), jnp.float32), 'Wo': glorot(ks[4]), 'bo': jnp.zeros((D,), jnp.float32), 'gamma': jnp.ones((D,), jnp.float32), 'beta': jnp.zeros((D,), jnp.float32)}
    _L0_attn_in = _L0_attn_setup()

    def _L0_ffn_setup():
        import jax, jax.numpy as jnp
        import numpy as np
        BLOCK = 16
        _GRID = jnp.array([0.0, 0.5, 1.0, 1.5, 2.0, 3.0, 4.0, 6.0], dtype=jnp.float32)
        _MID = jnp.array([0.25, 0.75, 1.25, 1.75, 2.5, 3.5, 5.0], dtype=jnp.float32)

        def fp4_quant_dequant(x):
            shape = x.shape
            xb = x.reshape(shape[:-1] + (shape[-1] // BLOCK, BLOCK))
            scale = jnp.max(jnp.abs(xb), axis=-1, keepdims=True) / 6.0
            scale = jnp.maximum(scale, jnp.float32(1e-12))
            xn = xb / scale
            idx = jnp.searchsorted(_MID, jnp.abs(xn))
            q = _GRID[idx] * jnp.sign(xn) * scale
            return q.reshape(shape)

        def fp4_linear(x, w):
            xq = fp4_quant_dequant(x)
            wq = fp4_quant_dequant(w)
            return jnp.einsum('bsk,nk->bsn', xq, wq)
        key = jax.random.key(seed)
        k1, k2, k3, k4 = jax.random.split(key, 4)
        H, I = (256, 704)
        x = jax.random.normal(k1, (4, 1024, H), dtype=jnp.float32)
        w_gate = jax.random.normal(k2, (I, H), dtype=jnp.float32) * 0.02
        w_up = jax.random.normal(k3, (I, H), dtype=jnp.float32) * 0.02
        w_down = jax.random.normal(k4, (H, I), dtype=jnp.float32) * 0.02
        return {'x': x, 'w_gate': w_gate, 'w_up': w_up, 'w_down': w_down}
    _L0_ffn_in = _L0_ffn_setup()
    _d = {'L0_attn_x': _L0_attn_in['x'], 'L0_attn_Wq': _L0_attn_in['Wq'], 'L0_attn_bq': _L0_attn_in['bq'], 'L0_attn_Wk': _L0_attn_in['Wk'], 'L0_attn_bk': _L0_attn_in['bk'], 'L0_attn_Wv': _L0_attn_in['Wv'], 'L0_attn_bv': _L0_attn_in['bv'], 'L0_attn_Wo': _L0_attn_in['Wo'], 'L0_attn_bo': _L0_attn_in['bo'], 'L0_attn_gamma': _L0_attn_in['gamma'], 'L0_attn_beta': _L0_attn_in['beta'], 'L0_ffn_w_gate': _L0_ffn_in['w_gate'], 'L0_ffn_w_up': _L0_ffn_in['w_up'], 'L0_ffn_w_down': _L0_ffn_in['w_down']}
    _x0 = _d['L0_attn_x']
    _d['L0_attn_x'] = jax.random.normal(jax.random.fold_in(jax.random.key(seed), 1), (8, 1024, 256), dtype=_x0.dtype)
    del _x0
    return _d

def reference(L0_attn_x, L0_attn_Wq, L0_attn_bq, L0_attn_Wk, L0_attn_bk, L0_attn_Wv, L0_attn_bv, L0_attn_Wo, L0_attn_bo, L0_attn_gamma, L0_attn_beta, L0_ffn_w_gate, L0_ffn_w_up, L0_ffn_w_down):

    def _L0_attn_ref(x, Wq, bq, Wk, bk, Wv, bv, Wo, bo, gamma, beta):
        import jax, jax.numpy as jnp
        import numpy as np
        B, S, D, H = (2, 512, 256, 16)
        DEPTH = D // H
        EPS = 1e-06

        def _split_heads(t):
            b, s, _ = t.shape
            return t.reshape(b, s, H, DEPTH).transpose(0, 2, 1, 3)
        b, s, d = x.shape
        q = _split_heads(x @ Wq + bq)
        k = _split_heads(x @ Wk + bk)
        v = _split_heads(x @ Wv + bv)
        q = jax.nn.elu(q) + 1.0
        k = jax.nn.elu(k) + 1.0
        k = k / jnp.sqrt(jnp.sum(k * k, axis=-1, keepdims=True) + EPS)
        scores = jnp.einsum('bhqd,bhkd->bhqk', q, k)
        attn = jnp.einsum('bhqk,bhkd->bhqd', scores, v)
        attn = attn.transpose(0, 2, 1, 3).reshape(b, s, d)
        out = attn @ Wo + bo
        y = x + out
        mu = jnp.mean(y, axis=-1, keepdims=True)
        var = jnp.mean(jnp.square(y - mu), axis=-1, keepdims=True)
        return (y - mu) / jnp.sqrt(var + EPS) * gamma + beta

    def _L0_ffn_ref(x, w_gate, w_up, w_down):
        import jax, jax.numpy as jnp
        import numpy as np
        BLOCK = 16
        _GRID = jnp.array([0.0, 0.5, 1.0, 1.5, 2.0, 3.0, 4.0, 6.0], dtype=jnp.float32)
        _MID = jnp.array([0.25, 0.75, 1.25, 1.75, 2.5, 3.5, 5.0], dtype=jnp.float32)

        def fp4_quant_dequant(x):
            shape = x.shape
            xb = x.reshape(shape[:-1] + (shape[-1] // BLOCK, BLOCK))
            scale = jnp.max(jnp.abs(xb), axis=-1, keepdims=True) / 6.0
            scale = jnp.maximum(scale, jnp.float32(1e-12))
            xn = xb / scale
            idx = jnp.searchsorted(_MID, jnp.abs(xn))
            q = _GRID[idx] * jnp.sign(xn) * scale
            return q.reshape(shape)

        def fp4_linear(x, w):
            xq = fp4_quant_dequant(x)
            wq = fp4_quant_dequant(w)
            return jnp.einsum('bsk,nk->bsn', xq, wq)
        gate = fp4_linear(x, w_gate)
        y = fp4_linear(x, w_up)
        h = jax.nn.silu(gate) * y
        return fp4_linear(h, w_down)
    x = L0_attn_x
    x = _layernorm(x + _L0_attn_ref(x, L0_attn_Wq, L0_attn_bq, L0_attn_Wk, L0_attn_bk, L0_attn_Wv, L0_attn_bv, L0_attn_Wo, L0_attn_bo, L0_attn_gamma, L0_attn_beta), axis=-1)
    x = _layernorm(x + _L0_ffn_ref(x, L0_ffn_w_gate, L0_ffn_w_up, L0_ffn_w_down), axis=-1)
    return x

_drawn_inputs = setup_inputs


def setup_inputs(seed=0):
    import zlib

    import numpy as np

    out = dict(_drawn_inputs(seed))
    spreads = {'L0_attn_bq': (0.0, 0.603),
     'L0_attn_bk': (0.0, 0.8),
     'L0_attn_bv': (0.0, 0.1),
     'L0_attn_bo': (0.0, 0.8),
     'L0_attn_gamma': (1.0, 0.2),
     'L0_attn_beta': (0.0, 0.1)}
    factors = {}
    for name, (base, spread) in spreads.items():
        noise = np.random.default_rng([zlib.crc32(name.encode()), seed]).standard_normal(out[name].shape)
        drawn = base * np.exp(spread * noise) if base else spread * noise
        out[name] = jnp.asarray(drawn.astype(out[name].dtype))
    for name, factor in factors.items():
        out[name] = (out[name] * factor).astype(out[name].dtype)
    return out
```

```python
from contextlib import ExitStack

import concourse.bass as bass
from concourse import mybir

F32 = mybir.dt.float32
F32R = mybir.dt.float32r
F16 = mybir.dt.float16
BF16 = mybir.dt.bfloat16
U16 = mybir.dt.uint16
U32 = mybir.dt.uint32
I32 = mybir.dt.int32
ALU = mybir.AluOpType
ACT = mybir.ActivationFunctionType
AX = mybir.AxisListType

P = 128
START = 1
BLK = 16
HD = 16
EPS_K = 1e-6
EPS_LN = 1e-5
SCALE_MIN = 1e-12
NUDGE = 1.0 + 2.0 ** -21
F16_ONE = 2.0 ** -14
ROUND_HALF = 0x100
ROUND_MASK = 0xFE00


def after(eng, sem, count):
    if not (isinstance(count, int) and count <= 0):
        eng.wait_ge(sem, count)


def build(nc, x, Wq, bq, Wk, bk, Wv, bv, Wo, bo, gamma, beta, w_gate, w_up, w_down, out):
    B, S, D = x.shape
    I = w_gate.shape[0]
    KT = D // P
    TPB = S // P
    T = B * TPB
    HALF = TPB // 2
    NP = TPB // 2
    IH = I // 2
    DB, IB = D // BLK, I // BLK
    DT = [(128 * i, 128) for i in range(4)] + [(512, 96), (608, 96)]
    assert (D, TPB) == (256, 8) and I == 704

    x_rows = x.rearrange("b (p j) d -> (b p) (j d)", j=TPB)
    out_rows = out.rearrange("b (p j) d -> (b p) (j d)", j=TPB)

    with ExitStack() as ctx:
        def sb(name, shape, dt=F32):
            return ctx.enter_context(nc.sbuf_tensor(name, shape, dt))

        def sem(name):
            return ctx.enter_context(nc.semaphore(name))

        resid = sb("resid", [P, T, DB, BLK])
        ident = sb("ident", [P, P])
        actT_hi = sb("actT_hi", [P, 2048], F32R)
        actT_lo = sb("actT_lo", [P, 2048], F32R)
        wkv_hi, wkv_lo = (sb(f"wkv_{n}", [P, KT, 2 * D], F32R) for n in ("hi", "lo"))
        wq_hi, wq_lo = (sb(f"wq_{n}", [P, KT, D], F32R) for n in ("hi", "lo"))
        wo_sb = sb("wo_sb", [P, KT, D])
        wgu_hi, wgu_lo = (sb(f"wgu_{n}", [P, KT, 2 * I], F32R) for n in ("hi", "lo"))
        wd_hi, wd_lo = (sb(f"wd_{n}", [P, len(DT), D], F32R) for n in ("hi", "lo"))
        headmask = sb("headmask", [P, P])
        bkv_b = sb("bkv_b", [P, 2 * D])
        bq_c = sb("bq_c", [P, KT])
        bo_b, gamma_b, cb_b = (sb(n, [P, D]) for n in ("bo_b", "gamma_b", "cb_b"))
        mhalf = sb("mhalf", [P, 1])
        eps_k = sb("eps_k", [P, 1])
        eps_ln = sb("eps_ln", [P, 1])

        arena = sb("arena", [P, 18200])
        at = [0]

        def take(words):
            at[0] += words
            assert at[0] <= 18200, at[0]
            return arena[:, at[0] - words:at[0]]

        xin = take(TPB * D).rearrange("p (j d) -> p j d", d=D)
        kvb = take(3 * 2 * 2 * D).rearrange("p (r j c) -> p r j c", r=3, j=2)
        kexp = take(2 * D).rearrange("p (j c) -> p j c", j=2)
        krelu = take(2 * D).rearrange("p (j c) -> p j c", j=2)
        kf = take(2 * 2 * D).rearrange("p (s n) -> p s n", s=2)
        khat = take(2 * 2 * D).rearrange("p (s j c) -> p s j c", s=2, j=2)
        kvt = take(KT * P).rearrange("p (m d) -> p m d", m=KT)
        mo = take(KT * D).rearrange("p (m d) -> p m d", m=KT)
        qexp = take(2 * 512).rearrange("p (s n) -> p s n", s=2)
        qrelu = take(2 * 512).rearrange("p (s n) -> p s n", s=2)
        qfT = take(KT * S).rearrange("p (m n) -> p m n", m=KT)
        y1 = take(2 * 2 * D).rearrange("p (s j d) -> p s j d", s=2, j=2)
        z1 = take(2 * D).rearrange("p (j d) -> p j d", j=2)
        w1 = take(2 * 2 * D).rearrange("p (s j d) -> p s j d", s=2, j=2)
        xbo = take(TPB * D).rearrange("p (j d) -> p j d", d=D)
        ssq = take(32)
        klog = take(32)
        kseed = take(32)
        ku, kv_ = take(32), take(32)
        knorm = take(64).rearrange("p (s n) -> p s n", s=2)
        st1, st2 = (take(12).rearrange("p (j n) -> p j n", j=2) for _ in range(2))
        mv1, mv2 = (take(4).rearrange("p (j n) -> p j n", j=2) for _ in range(2))
        log1, seed1, u1, v1, rstd1, nmr1 = (take(2) for _ in range(6))
        log2, seed2, u2, v2, rstd2 = (take(2) for _ in range(5))
        at[0] = 0
        xam, xsn, xs14, xinv = (take(2 * DB).rearrange("p (s n) -> p s n", s=2) for _ in range(4))
        xy = take(2 * D).rearrange("p (s n) -> p s n", s=2)
        xq = take(D).rearrange("p (s n) -> p s n", s=2)
        xa = take(2 * D).rearrange("p (s n) -> p s n", s=2)
        gact = take(2 * IH).rearrange("p (s n) -> p s n", s=2)
        h = take(2 * I).rearrange("p (s n) -> p s n", s=2)
        ham, hsn, hs14, hinv = (take(2 * IB).rearrange("p (s n) -> p s n", s=2) for _ in range(4))
        hy = take(2 * I).rearrange("p (s n) -> p s n", s=2)
        hq = take(I).rearrange("p (s n) -> p s n", s=2)
        ha = take(2 * I).rearrange("p (s n) -> p s n", s=2)
        r3 = take(2 * D).rearrange("p (s d) -> p s d", s=2)
        ob = take(2 * 2 * D).rearrange("p (s j d) -> p s j d", s=2, j=2)
        st3 = take(12).rearrange("p (s n) -> p s n", s=2)
        mv3 = take(4).rearrange("p (s n) -> p s n", s=2)
        ve3, rstd3 = take(2), take(2)
        scratch = resid[:, :, :, :].rearrange("p t g e -> p (t g e)")
        NW = 2 * I * D // P + D * I // P
        wraw, wy, wa = (scratch[:, i * NW:(i + 1) * NW] for i in range(3))
        wqn = scratch[:, 3 * NW:3 * NW + NW // 2].bitcast(F16)
        o = 3 * NW + NW // 2
        wkv_st = scratch[:, o:o + KT * 2 * D].rearrange("p (k n) -> p k n", k=KT)
        wq_st = scratch[:, o + 1024:o + 1024 + KT * D].rearrange("p (k n) -> p k n", k=KT)
        wam, wsn, ws14, winv = (arena[:, 18200 - (i + 1) * 264:18200 - i * 264] for i in range(4))

        def halves(y):
            return y.bitcast(BF16).rearrange("p (n two) -> p n two", two=2)[:, :, 1]

        def blocks(a):
            return a.rearrange("p (g e) -> p g e", e=BLK)

        def each(a):
            return a.unsqueeze(2).broadcast_to([P, a.shape[1], BLK])

        xT_hi, xT_lo = (a[:, :].rearrange("p (k n) -> p k n", k=KT) for a in (actT_hi, actT_lo))
        xqT_hi, xqT_lo = (a[:, 0:512].rearrange("p (s k n) -> p s k n", s=2, k=KT) for a in (actT_hi, actT_lo))
        hqT_hi, hqT_lo = (a[:, 512:2048].rearrange("p (s k n) -> p s k n", s=2, k=6) for a in (actT_hi, actT_lo))

        def f32(a):
            return a.bitcast(F32)

        ps = [ctx.enter_context(nc.psum_tensor(f"bank{i}", [P, 512], F32)) for i in range(8)]

        consts_in, watt_in, wffn_in = sem("consts_in"), sem("watt_in"), sem("wffn_in")
        consts_set, small_set = sem("consts_set"), sem("small_set")
        watt_hi, watt_lo = sem("watt_hi"), sem("watt_lo")
        w_amax, w_small, w_small2, w_scaled, w_f16, w_half, w_rounded, w_deq, mask_s = (
            sem(n) for n in ("w_amax", "w_nudged", "w_scales", "w_scaled", "w_f16", "w_half", "w_rounded", "w_deq", "mask"))
        wT_ps, wT_hi, wT_lo = sem("wT_ps"), sem("wT_hi"), sem("wT_lo")
        x_in = [sem(f"x_in{i}") for i in range(2)]
        xT_ps, xT_hi_s, xT_lo_s = sem("xT_ps"), sem("xT_hi_done"), sem("xT_lo_done")
        kv_ps, kv_biased, k_act, k_feat, k_sq, k_ssq, k_seed, k_u, k_v, k_norm, k_hat, kv_acc = (
            sem(n) for n in ("kv_ps", "kv_biased", "k_act", "k_feat", "k_sq", "k_ssq", "k_seed", "k_u", "k_v",
                             "k_norm", "k_hat", "kv_acc"))
        kvt_s, mo_ps, mo_sb = sem("kvt_done"), sem("mo_ps"), sem("mo_sb")
        q_ps, q_act, q_feat = sem("q_ps"), sem("q_act"), sem("q_feat")
        x_plus = sem("x_plus")
        o_ps, y1_s, st1_s, mv1_s, log1_s, seed1_s, u1_s, v1_s, rstd1_s, nmr1_s, z1_s, zg_s, zx_s, w1_s = (
            sem(n) for n in ("o_ps", "y1_done", "st1_done", "mv1_done", "log1_done", "seed1_done", "u1_done", "v1_done",
                             "rstd1_done", "nmr1_done", "z1_done", "zg_done", "zx_done", "w1_done"))
        st2_s, mv2_s, log2_s, seed2_s, u2_s, v2_s, rstd2_s, x1_s = (
            sem(n) for n in ("st2_done", "mv2_done", "log2_done", "seed2_done", "u2_done", "v2_done", "rstd2_done",
                             "x1_done"))
        klog_s = sem("klog_done")
        phase_a = sem("phase_a")
        xam_s, xsn_s, xsc_s, xy_s, xf_s, xh_s, xr_s, xa_s = (
            sem(n) for n in ("xam_done", "xsn_done", "xscale_done", "xy_done", "xf16_done", "xhalf_done", "xround_done",
                             "xdeq_done"))
        tx_ps, tx_hi, tx_lo = sem("tx_ps"), sem("tx_hi"), sem("tx_lo")
        gu_ps, g_act, h_s = sem("gu_ps"), sem("g_act"), sem("h_done")
        ham_s, hsn_s, hsc_s, hy_s, hf_s, hh_s, hr_s, ha_s = (
            sem(n) for n in ("ham_done", "hsn_done", "hscale_done", "hy_done", "hf16_done", "hhalf_done", "hround_done",
                             "hdeq_done"))
        th_ps, th_hi, th_lo = sem("th_ps"), sem("th_hi"), sem("th_lo")
        dn_ps, r3_s, st3_s, mv3_s, ve3_s, rstd3_s, ob_s = (
            sem(n) for n in ("dn_ps", "r3_done", "st3_done", "mv3_done", "ve3_done", "rstd3_done", "ob_done"))
        stored = [sem(f"stored{i}") for i in range(2)]

        GU_TILES = 2 * I // P
        GUW = GU_TILES * D
        CH = [(0, 6 * D), (6 * D, GUW), (GUW, NW)]
        WG = []
        for tiles in ((0, 1, 2, 3), (4, 5), (6, 7, 8, 9), (10,)):
            for k in range(KT):
                n0, n1 = tiles[0] * P, (tiles[-1] + 1) * P
                WG.append((0 if tiles[0] < 6 else 1, [(i * D + k * P, P) for i in tiles],
                           wgu_hi[:, k, n0:n1], wgu_lo[:, k, n0:n1]))
        for n in range(KT):
            for k0, k1 in ((0, 4), (4, 6)):
                rows = DT[k0][1]
                WG.append((2, [(GUW + n * I + s, w) for s, w in DT[k0:k1]],
                           wd_hi[0:rows, k0:k1, n * P:(n + 1) * P], wd_lo[0:rows, k0:k1, n * P:(n + 1) * P]))

        def wg_view(g):
            _, cols, hi, _ = WG[g]
            v = ps[g % 8][0:cols[0][1], 0:len(cols) * P]
            return v if len(hi.shape) == 2 else v.rearrange("p (k n) -> p k n", n=P)

        block = ctx.enter_context(nc.Block())

        @block.sync
        def _(sp):
            for s in (xT_lo_s, kv_biased, kvt_s, y1_s, k_hat, q_feat, kv_acc, w1_s):
                sp.sem_inc(s, START)
            for hf in range(2):
                sp.dma_start(xin[:, hf * HALF:(hf + 1) * HALF, :],
                             x_rows[0:P, hf * HALF * D:(hf + 1) * HALF * D]).then_inc(x_in[hf], 16)
            sp.dma_start(wkv_st[:, :, 0:D], Wk.rearrange("(k p) n -> p k n", p=P)).then_inc(watt_in, 16)
            sp.dma_start(wkv_st[:, :, D:2 * D], Wv.rearrange("(k p) n -> p k n", p=P)).then_inc(watt_in, 16)
            sp.dma_start(wq_st, Wq.rearrange("(k p) n -> p k n", p=P)).then_inc(watt_in, 16)
            gu = wraw[:, 0:GUW].rearrange("p (i d) -> p i d", d=D)
            whole, part = I // P, I % P
            sp.dma_start(gu[:, 0:whole, :], w_gate[0:whole * P, :].rearrange("(i p) d -> p i d", p=P)).then_inc(wffn_in, 16)
            sp.dma_start(gu[0:part, whole, :], w_gate[whole * P:I, :]).then_inc(wffn_in, 16)
            sp.dma_start(gu[part:P, whole, :], w_up[0:P - part, :]).then_inc(wffn_in, 16)
            sp.dma_start(gu[:, whole + 1:GU_TILES, :],
                         w_up[P - part:I, :].rearrange("(i p) d -> p i d", p=P)).then_inc(wffn_in, 16)
            sp.dma_start(wraw[:, GUW:NW].rearrange("p (n c) -> p n c", n=KT),
                         w_down.rearrange("(n p) c -> p n c", p=P)).then_inc(wffn_in, 16)

            with sp.Fori(0, B - 1) as b:
                t0 = b * TPB
                for hf in range(2):
                    sp.wait_ge(xT_ps, t0 + (HALF * (hf + 1)))
                    sp.wait_ge(x_plus, t0 + (HALF * (hf + 1)))
                    sp.dma_start(xin[:, hf * HALF:(hf + 1) * HALF, :],
                                 x_rows[bass.ds(b * P + P, P), hf * HALF * D:(hf + 1) * HALF * D]
                                 ).then_inc(x_in[hf], 16)

            with sp.Fori(0, B) as b:
                t0 = b * TPB
                for r in range(NP):
                    sp.wait_ge(ob_s, t0 + (2 * r + 2))
                    sp.dma_start(out_rows[bass.ds(b * P, P), r * 2 * D:(r + 1) * 2 * D],
                                 ob[:, r % 2, :, :].rearrange("p j d -> p (j d)")).then_inc(stored[r % 2], 16)
            for i in range(2):
                sp.wait_ge(stored[i], 16 * T // 4)

        @block.tensor
        def _(pe):
            pe.wait_ge(consts_set, 2)
            for g, (chunk, cols, _, _) in enumerate(WG):
                pe.wait_ge(w_deq, chunk + 1)
                after(pe, wT_lo, g - 7)
                for i, (c, w) in enumerate(cols):
                    last = nc.tensor.transpose(ps[g % 8][0:w, i * P:(i + 1) * P], wa[:, c:c + w], ident[:, :])
                last.then_inc(wT_ps, 1)
            pe.wait_ge(wT_lo, len(WG))

            def x_transpose(t0, r):
                for j in (2 * r, 2 * r + 1):
                    if j % HALF == 0:
                        pe.wait_ge(x_in[j // HALF], t0 * 2 + 16)
                    pe.wait_ge(xT_lo_s, t0 + START if j == 0 else t0 + (START + j - 1))
                    for k in range(KT):
                        last = nc.tensor.transpose(ps[j % 2][:, k * P:(k + 1) * P], xin[:, j, k * P:(k + 1) * P],
                                                   ident[:, :])
                    last.then_inc(xT_ps, 1)

            def split_product(dst, stat, mov, n):
                for k in range(n):
                    (sh, sl), (mh, ml) = stat(k), mov(k)
                    nc.tensor.matmul(dst, sl, mh, start=(k == 0), stop=False)
                    nc.tensor.matmul(dst, sh, ml, start=False, stop=False)
                    last = nc.tensor.matmul(dst, sh, mh, start=False, stop=(k == n - 1))
                return last

            def kv_project(t0, r):
                for j in (2 * r, 2 * r + 1):
                    pe.wait_ge(xT_lo_s, t0 + (START + j + 1))
                    pe.wait_ge(kv_biased, t0 + START if j == 0 else t0 + (START + j - 1))
                    c = slice(j * P, (j + 1) * P)
                    split_product(ps[2 + j % 2][:, :], lambda k: (xT_hi[:, k, c], xT_lo[:, k, c]),
                                  lambda k: (wkv_hi[:, k, :], wkv_lo[:, k, :]), KT).then_inc(kv_ps, 1)

            def kv_accumulate(t0, r):
                pe.wait_ge(k_hat, t0 + (START + 2 * r + 2))
                if r == 0:
                    pe.wait_ge(kvt_s, t0 + START)
                for jj in range(2):
                    j = 2 * r + jj
                    for m in range(KT):
                        last = nc.tensor.matmul(ps[4 + m][:, 0:P], kvb[:, r % 3, jj, D + m * P:D + (m + 1) * P],
                                                khat[:, r % 2, jj, m * P:(m + 1) * P],
                                                start=(j == 0), stop=(j == TPB - 1))
                    last.then_inc(kv_acc, 1)

            def q_project(t0, g):
                for m in range(KT):
                    u = KT * g + m
                    if u < 2:
                        pe.wait_ge(y1_s, t0 + START)
                    else:
                        pe.wait_ge(q_act, t0 + (2 * (u - 1)))
                    c = slice(g * 512, (g + 1) * 512)
                    split_product(ps[6 + u % 2][:, :],
                                  lambda k: (wq_hi[:, k, m * P:(m + 1) * P], wq_lo[:, k, m * P:(m + 1) * P]),
                                  lambda k: (xT_hi[:, k, c], xT_lo[:, k, c]), KT).then_inc(q_ps, 2)

            with pe.Fori(0, B) as b:
                t0 = b * TPB
                x_transpose(t0, 0)
                x_transpose(t0, 1)
                pe.wait_ge(watt_lo, 3)
                kv_project(t0, 0)
                x_transpose(t0, 2)
                kv_project(t0, 1)
                x_transpose(t0, 3)
                kv_project(t0, 2)
                kv_accumulate(t0, 0)
                kv_project(t0, 3)
                kv_accumulate(t0, 1)
                q_project(t0, 0)
                kv_accumulate(t0, 2)
                q_project(t0, 1)
                kv_accumulate(t0, 3)
                for m in range(KT):
                    pe.wait_ge(kvt_s, t0 + (START + 4 * (m + 1)))
                    pe.wait_ge(q_act, t0 + (6 + 2 * m))
                    nc.tensor.matmul(ps[6 + m][:, 0:D], kvt[:, m, :], wo_sb[:, m, :],
                                     start=True, stop=True).then_inc(mo_ps, 4)
                for j in range(TPB):
                    if j == 0:
                        pe.wait_ge(mo_sb, t0 + TPB)
                    if j % HALF == 0:
                        pe.wait_ge(q_feat, t0 + (START + HALF * (j // HALF + 1)))
                    if j >= 2:
                        pe.wait_ge(y1_s, t0 + (START + j - 1))
                    for m in range(KT):
                        last = nc.tensor.matmul(ps[6 + j % 2][:, 0:D], qfT[:, m, j * P:(j + 1) * P], mo[:, m, :],
                                                start=(m == 0), stop=(m == KT - 1))
                    last.then_inc(o_ps, 1)

            nc.tensor.drain().then_inc(phase_a, 1)
            pe.wait_ge(phase_a, 4)

            def x_turn(t, s):
                pe.wait_ge(xa_s, t + 1)
                after(pe, tx_lo, t)
                for k in range(KT):
                    last = nc.tensor.transpose(ps[6][:, k * P:(k + 1) * P], xa[:, s, k * P:(k + 1) * P], ident[:, :])
                last.then_inc(tx_ps, 1)

            def gate_up(t, s, half):
                if half == 0:
                    pe.wait_ge(tx_lo, t + 1)
                after(pe, h_s, 2 * t - 1 + half)
                for w in range(2):
                    c = slice(w * I + half * IH, w * I + (half + 1) * IH)
                    last = split_product(ps[2 * half + w][:, 0:IH], lambda k: (xqT_hi[:, s, k, :], xqT_lo[:, s, k, :]),
                                         lambda k: (wgu_hi[:, k, c], wgu_lo[:, k, c]), KT)
                last.then_inc(gu_ps, 1)

            def h_turn(t, s):
                pe.wait_ge(ha_s, t + 1)
                after(pe, th_lo, t)
                for k, (c, w) in enumerate(DT):
                    last = nc.tensor.transpose(ps[4 + k // 4][0:w, (k % 4) * P:(k % 4 + 1) * P], ha[:, s, c:c + w],
                                               ident[:, :])
                last.then_inc(th_ps, 1)

            def down(t, s):
                pe.wait_ge(th_lo, t + 1)
                after(pe, r3_s, t)
                rows = [w for _, w in DT]
                split_product(ps[7][:, 0:D], lambda k: (hqT_hi[0:rows[k], s, k, :], hqT_lo[0:rows[k], s, k, :]),
                              lambda k: (wd_hi[0:rows[k], k, :], wd_lo[0:rows[k], k, :]), len(DT)).then_inc(dn_ps, 1)

            def step(t, n, lo=-10, hi=10 ** 9):
                if 0 <= hi:
                    gate_up(t, n % 2, 0)
                if lo <= -2:
                    h_turn(t - 2, n % 2)
                if 1 <= hi:
                    x_turn(t + 1, (n + 1) % 2)
                if 0 <= hi:
                    gate_up(t, n % 2, 1)
                if lo <= -2:
                    down(t - 2, n % 2)

            x_turn(0, 0)
            for n in range(4):
                step(n, n, lo=-n)
            with pe.Fori(1, T // 4 - 1) as i:
                t = i * 4
                for n in range(4):
                    step(t + n, n)
            for n in range(T - 4, T + 2):
                step(n, n, hi=T - 1 - n)

        @block.scalar
        def _(act):
            act.dma_start(wo_sb[:, :, :], Wo.rearrange("(k p) n -> p k n", p=P)).then_inc(consts_in, 16)
            act.dma_start(bkv_b[:, 0:D], bk.partition_broadcast(P)).then_inc(consts_in, 16)
            act.dma_start(bkv_b[:, D:2 * D], bv.partition_broadcast(P)).then_inc(consts_in, 16)
            act.dma_start(bo_b[:, :], bo.partition_broadcast(P)).then_inc(consts_in, 16)
            act.dma_start(gamma_b[:, :], gamma.partition_broadcast(P)).then_inc(consts_in, 16)
            act.dma_start(cb_b[:, :], beta.partition_broadcast(P)).then_inc(consts_in, 16)
            act.dma_start(bq_c[:, :], bq.rearrange("(m p) -> p m", p=P), allow_slow_non_contiguous=True).then_inc(consts_in, 16)
            nc.scalar.preload_act_table_set("natural_log_exp_and_others")
            act.wait_ge(watt_in, 48)
            nc.scalar.activation(wkv_hi[:, :, :], wkv_st, ACT.Copy).then_inc(watt_hi, 1)
            nc.scalar.activation(wq_hi[:, :, :], wq_st, ACT.Copy).then_inc(watt_hi, 1)
            for c, (a, b) in enumerate(CH):
                act.wait_ge(w_scaled, c + 1)
                nc.scalar.activation(wqn[:, a:b], halves(wy[:, a:b]), ACT.Copy, scale=F16_ONE).then_inc(w_f16, 1)
            for g, (_, _, hi, _) in enumerate(WG):
                act.wait_ge(wT_ps, g + 1)
                nc.scalar.activation(hi, wg_view(g), ACT.Copy).then_inc(wT_hi, 1)
            act.wait_ge(consts_in, 7 * 16)
            act.wait_ge(small_set, 3)

            def x_high(t0, r):
                for j in (2 * r, 2 * r + 1):
                    act.wait_ge(xT_ps, t0 + (j + 1))
                    nc.scalar.activation(xT_hi[:, :, j * P:(j + 1) * P],
                                         ps[j % 2][:, 0:D].rearrange("p (k n) -> p k n", k=KT),
                                         ACT.Copy).then_inc(xT_hi_s, 1)

            def k_maps(t0, r):
                act.wait_ge(kv_biased, t0 + (START + 2 * r + 2))
                nc.scalar.activation(kexp, kvb[:, r % 3, :, 0:D], ACT.Exp)
                nc.scalar.activation(krelu, kvb[:, r % 3, :, 0:D], ACT.Relu).then_inc(k_act, 2)

            def k_squares(t0, r):
                act.wait_ge(k_feat, t0 + (2 * r + 2))
                nc.scalar.activation(kexp.rearrange("p j c -> p (j c)"), kf[:, r % 2, :], ACT.Square).then_inc(k_sq, 2)

            def k_seeds(t0, r):
                act.wait_ge(k_ssq, t0 + (2 * r + 2))
                nc.scalar.activation(klog, ssq, ACT.Ln, bias=eps_k[:, :]).then_inc(klog_s, 2)
                act.wait_ge(klog_s, t0 + (2 * r + 2))
                nc.scalar.activation(kseed, klog, ACT.Exp, scale=-0.5).then_inc(k_seed, 2)

            def q_maps(t0, u):
                act.wait_ge(q_ps, t0 + (2 * (u + 1)))
                act.wait_ge(q_feat, t0 + (START + 2 * (u - 1)) if u >= 2 else t0 + START)
                b = bq_c[:, u % KT:u % KT + 1]
                nc.scalar.activation(qexp[:, u % 2, :], ps[6 + u % 2][:, :], ACT.Exp, bias=b)
                nc.scalar.activation(qrelu[:, u % 2, :], ps[6 + u % 2][:, :], ACT.Relu, bias=b).then_inc(q_act, 2)

            def ln1_seed(t0, r):
                act.wait_ge(mv1_s, t0 + (2 * r + 2))
                nc.scalar.activation(log1, mv1[:, :, 1], ACT.Ln, bias=eps_k[:, :]).then_inc(log1_s, 2)
                act.wait_ge(log1_s, t0 + (2 * r + 2))
                nc.scalar.activation(seed1, log1, ACT.Exp, scale=-0.5).then_inc(seed1_s, 2)

            def ln1_apply(t0, r):
                act.wait_ge(nmr1_s, t0 + (2 * r + 2))
                for jj in range(2):
                    last = nc.scalar.activation(z1[:, jj, :], y1[:, r % 2, jj, :], ACT.Identity,
                                                scale=rstd1[:, jj:jj + 1], bias=nmr1[:, jj:jj + 1])
                last.then_inc(z1_s, 2)

            def ln2_seed(t0, r):
                act.wait_ge(mv2_s, t0 + (2 * r + 2))
                nc.scalar.activation(log2, mv2[:, :, 1], ACT.Ln, bias=eps_ln[:, :]).then_inc(log2_s, 2)
                act.wait_ge(log2_s, t0 + (2 * r + 2))
                nc.scalar.activation(seed2, log2, ACT.Exp, scale=-0.5).then_inc(seed2_s, 2)

            with act.Fori(0, B) as b:
                t0 = b * TPB
                x_high(t0, 0)
                x_high(t0, 1)
                for r in range(NP):
                    if r == 3:
                        q_maps(t0, 0)
                    k_maps(t0, r)
                    if r < 2:
                        x_high(t0, r + 2)
                    if r == 3:
                        q_maps(t0, 1)
                    k_squares(t0, r)
                    k_seeds(t0, r)
                q_maps(t0, 2)
                q_maps(t0, 3)
                for m in range(KT):
                    act.wait_ge(mo_ps, t0 + (4 * (m + 1)))
                    nc.scalar.activation(mo[:, m, :], ps[6 + m][:, 0:D], ACT.Copy).then_inc(mo_sb, 4)
                for r in range(NP + 1):
                    if r < NP:
                        ln1_seed(t0, r)
                    if r > 0:
                        ln2_seed(t0, r - 1)
                    if r < NP:
                        ln1_apply(t0, r)

            nc.scalar.drain().then_inc(phase_a, 1)
            nc.scalar.preload_act_table_set("silu_and_others")
            act.wait_ge(phase_a, 4)

            def x_f16(t, s):
                act.wait_ge(xy_s, t + 1)
                after(act, xa_s, t - 1)
                nc.scalar.activation(xq[:, s, :].bitcast(F16), halves(xy[:, s, :]), ACT.Copy,
                                     scale=F16_ONE).then_inc(xf_s, 1)

            def h_f16(t, s):
                act.wait_ge(hy_s, t + 1)
                after(act, ha_s, t - 1)
                nc.scalar.activation(hq[:, s, :].bitcast(F16), halves(hy[:, s, :]), ACT.Copy,
                                     scale=F16_ONE).then_inc(hf_s, 1)

            def x_hi(t, s):
                act.wait_ge(tx_ps, t + 1)
                after(act, gu_ps, 2 * t - 2)
                nc.scalar.activation(xqT_hi[:, s, :, :], ps[6][:, 0:D].rearrange("p (k n) -> p k n", k=KT),
                                     ACT.Copy).then_inc(tx_hi, 1)

            def h_hi(t, s):
                act.wait_ge(th_ps, t + 1)
                after(act, dn_ps, t - 1)
                for k0, k1, w in ((0, 4, 128), (4, 6, 96)):
                    nc.scalar.activation(hqT_hi[0:w, s, k0:k1, :],
                                         ps[4 + k0 // 4][0:w, 0:(k1 - k0) * P].rearrange("p (k n) -> p k n", n=P),
                                         ACT.Copy).then_inc(th_hi, 1)

            def silu(t, half):
                act.wait_ge(gu_ps, 2 * t + half + 1)
                after(act, h_s, 2 * t + half - 1)
                nc.scalar.activation(gact[:, half, :], ps[2 * half][:, 0:IH], ACT.Silu).then_inc(g_act, 1)

            def step(t, n, lo=-10, hi=10 ** 9):
                if lo <= -1 and -1 <= hi:
                    h_f16(t - 1, (n + 1) % 2)
                if 0 <= hi:
                    silu(t, 0)
                if lo <= -2:
                    h_hi(t - 2, n % 2)
                if 1 <= hi:
                    x_hi(t + 1, (n + 1) % 2)
                if 0 <= hi:
                    silu(t, 1)
                if 2 <= hi:
                    x_f16(t + 2, n % 2)

            x_f16(0, 0)
            x_hi(0, 0)
            x_f16(1, 1)
            for n in range(4):
                step(n, n, lo=-n)
            with act.Fori(1, T // 4 - 1) as i:
                t = i * 4
                for n in range(4):
                    step(t + n, n)
            for n in range(T - 4, T + 2):
                step(n, n, hi=T - 1 - n)

        @block.vector
        def _(dve):
            nc.vector.memset(mhalf[:, :], -0.5).then_inc(small_set, 1)
            nc.vector.memset(eps_k[:, :], EPS_K).then_inc(small_set, 1)
            nc.vector.memset(eps_ln[:, :], EPS_LN).then_inc(small_set, 1)
            for i, (lo, hi, st) in enumerate(((wkv_lo, wkv_hi, wkv_st), (wq_lo, wq_hi, wq_st))):
                dve.wait_ge(watt_hi, i + 1)
                nc.vector.tensor_tensor(lo[:, :, :], st, f32(hi[:, :, :]), ALU.subtract).then_inc(watt_lo, 1)
            dve.wait_ge(consts_in, 7 * 16)
            nc.vector.tensor_tensor(cb_b[:, :], cb_b[:, :], bo_b[:, :], ALU.subtract).then_inc(watt_lo, 1)
            dve.wait_ge(wffn_in, 5 * 16)

            def scales(src, am, sn, s14, inv, sem_am, sem_sn, sem_sc, v):
                nc.vector.tensor_reduce(am, src, AX.X, ALU.max, apply_absolute_value=True).then_inc(sem_am, 1)
                dve.wait_ge(sem_am, v)
                nc.vector.tensor_scalar(sn, am, NUDGE / 6.0, SCALE_MIN * NUDGE, ALU.mult, ALU.max).then_inc(sem_sn, 1)
                nc.vector.tensor_scalar(s14, am, 1.0 / 6.0 / F16_ONE, SCALE_MIN / F16_ONE, ALU.mult, ALU.max)
                dve.wait_ge(sem_sn, v)
                nc.vector.reciprocal(inv, sn).then_inc(sem_sc, 1)

            def half_up(q, sem_half, sem_round, v):
                nc.vector.tensor_scalar(q, q, ROUND_HALF, None, ALU.add).then_inc(sem_half, 1)
                dve.wait_ge(sem_half, v)
                nc.vector.tensor_scalar(q, q, ROUND_MASK, None, ALU.bitwise_and).then_inc(sem_round, 1)

            for c, (a, b) in enumerate(CH):
                g = slice(a // BLK, b // BLK)
                scales(blocks(wraw[:, a:b]), wam[:, g], wsn[:, g], ws14[:, g], winv[:, g],
                       w_amax, w_small, w_small2, c + 1)
            for c, (a, b) in enumerate(CH):
                dve.wait_ge(w_f16, c + 1)
                half_up(wqn[:, a:b].bitcast(U16), w_half, w_rounded, c + 1)
            for g, (_, _, hi, lo) in enumerate(WG):
                dve.wait_ge(wT_hi, g + 1)
                nc.vector.tensor_tensor(lo, wg_view(g), f32(hi), ALU.subtract).then_inc(wT_lo, 1)
            dve.wait_ge(consts_set, 4)

            def x_low(t0, r):
                for j in (2 * r, 2 * r + 1):
                    c = slice(j * P, (j + 1) * P)
                    dve.wait_ge(xT_hi_s, t0 + (j + 1))
                    nc.vector.tensor_tensor(xT_lo[:, :, c], ps[j % 2][:, 0:D].rearrange("p (k n) -> p k n", k=KT),
                                            f32(xT_hi[:, :, c]), ALU.subtract).then_inc(xT_lo_s, 1)

            def kv_bias(t0, r):
                if r == 3:
                    dve.wait_ge(kv_acc, t0 + (START + 2))
                for jj in range(2):
                    j = 2 * r + jj
                    dve.wait_ge(kv_ps, t0 + (j + 1))
                    nc.vector.tensor_tensor(kvb[:, r % 3, jj, :], ps[2 + j % 2][:, :], bkv_b[:, :],
                                            ALU.add).then_inc(kv_biased, 1)

            def k_features(t0, r):
                dve.wait_ge(k_act, t0 + (2 * r + 2))
                dve.wait_ge(k_hat, t0 + (START + 2 * r - 2) if r >= 2 else t0 + START)
                nc.vector.scalar_tensor_tensor(out=kf[:, r % 2, :], in0=kexp.rearrange("p j c -> p (j c)"), scalar=1.0,
                                               in1=krelu.rearrange("p j c -> p (j c)"), op0=ALU.min,
                                               op1=ALU.add).then_inc(k_feat, 2)

            def k_sums(t0, r):
                dve.wait_ge(k_sq, t0 + (2 * r + 2))
                nc.vector.tensor_reduce(ssq, kexp.rearrange("p j (g e) -> p (j g) e", e=HD), AX.X,
                                        ALU.add).then_inc(k_ssq, 2)

            def root(v, eps, seed, var, a, b, dst, s_seed, s_a, s_b, s_dst):
                dve.wait_ge(s_seed, v)
                nc.vector.scalar_tensor_tensor(out=a, in0=var, scalar=eps, in1=seed, op0=ALU.add,
                                               op1=ALU.mult).then_inc(s_a, 2)
                dve.wait_ge(s_a, v)
                nc.vector.scalar_tensor_tensor(out=b, in0=a, scalar=-0.5, in1=seed, op0=ALU.mult,
                                               op1=ALU.mult).then_inc(s_b, 2)
                dve.wait_ge(s_b, v)
                nc.vector.scalar_tensor_tensor(out=dst, in0=b, scalar=1.5, in1=seed, op0=ALU.add,
                                               op1=ALU.mult).then_inc(s_dst, 2)

            def k_norms(t0, r):
                root(t0 + (2 * r + 2), EPS_K, kseed, ssq, ku, kv_, knorm[:, r % 2, :], k_seed, k_u, k_v, k_norm)

            def q_features(t0, u):
                dve.wait_ge(q_act, t0 + (2 * (u + 1)))
                nc.vector.scalar_tensor_tensor(out=qfT[:, u % KT, (u // KT) * 512:(u // KT + 1) * 512],
                                               in0=qexp[:, u % 2, :], scalar=1.0, in1=qrelu[:, u % 2, :],
                                               op0=ALU.min, op1=ALU.add).then_inc(q_feat, 2)

            def ln1_stats(t0, r):
                for jj in range(2):
                    j = 2 * r + jj
                    dve.wait_ge(o_ps, t0 + (j + 1))
                    if jj == 0:
                        dve.wait_ge(x_plus, t0 + (HALF * (j // HALF + 1)))
                    nc.vector.tensor_tensor(y1[:, r % 2, jj, :], ps[6 + j % 2][:, 0:D], xbo[:, j, :],
                                            ALU.add).then_inc(y1_s, 1)
                for jj in range(2):
                    dve.wait_ge(y1_s, t0 + (START + 2 * r + jj + 1))
                    nc.vector.bn_stats(st1[:, jj, :], y1[:, r % 2, jj, :]).then_inc(st1_s, 1)
                for jj in range(2):
                    dve.wait_ge(st1_s, t0 + (2 * r + jj + 1))
                    nc.vector.nop(nofuse=True)
                    nc.vector.bn_aggr(mv1[:, jj, :], st1[:, jj, :]).then_inc(mv1_s, 1)

            def ln1_norm(t0, r):
                v = t0 + (2 * r + 2)
                root(v, EPS_K, seed1, mv1[:, :, 1], u1, v1, rstd1, seed1_s, u1_s, v1_s, rstd1_s)
                dve.wait_ge(rstd1_s, v)
                nc.vector.scalar_tensor_tensor(out=nmr1, in0=mv1[:, :, 0], scalar=-1.0, in1=rstd1, op0=ALU.mult,
                                               op1=ALU.mult).then_inc(nmr1_s, 2)

            def ln2_stats(t0, r):
                dve.wait_ge(w1_s, t0 + (START + 2 * r + 2))
                for jj in range(2):
                    nc.vector.bn_stats(st2[:, jj, :], w1[:, r % 2, jj, :]).then_inc(st2_s, 1)
                for jj in range(2):
                    dve.wait_ge(st2_s, t0 + (2 * r + jj + 1))
                    nc.vector.nop(nofuse=True)
                    nc.vector.bn_aggr(mv2[:, jj, :], st2[:, jj, :]).then_inc(mv2_s, 1)

            def ln2_apply(t0, r):
                v = t0 + (2 * r + 2)
                root(v, EPS_LN, seed2, mv2[:, :, 1], u2, v2, rstd2, seed2_s, u2_s, v2_s, rstd2_s)
                dve.wait_ge(rstd2_s, v)
                for jj in range(2):
                    nc.vector.tensor_scalar(resid[:, bass.ds(t0 + (2 * r + jj), 1), :, :].rearrange("p t g e -> p (t g e)"),
                                            w1[:, r % 2, jj, :], mv2[:, jj, 0:1], rstd2[:, jj:jj + 1],
                                            ALU.subtract, ALU.mult).then_inc(x1_s, 1)

            with dve.Fori(0, B) as b:
                t0 = b * TPB
                x_low(t0, 0)
                x_low(t0, 1)
                kv_bias(t0, 0)
                for r in range(NP):
                    if r == 3:
                        q_features(t0, 0)
                    if r < 2:
                        x_low(t0, r + 2)
                    k_features(t0, r)
                    if r < 3:
                        kv_bias(t0, r + 1)
                    if r == 3:
                        q_features(t0, 1)
                    k_sums(t0, r)
                    k_norms(t0, r)
                q_features(t0, 2)
                q_features(t0, 3)
                for m in range(KT):
                    dve.wait_ge(kv_acc, t0 + (START + TPB))
                    nc.vector.tensor_tensor(kvt[:, m, :], ps[4 + m][:, 0:P], headmask[:, :],
                                            ALU.mult).then_inc(kvt_s, 4)
                for r in range(NP + 1):
                    if r < NP:
                        ln1_stats(t0, r)
                    if r > 0:
                        ln2_stats(t0, r - 1)
                    if r < NP:
                        ln1_norm(t0, r)
                    if r > 0:
                        ln2_apply(t0, r - 1)

            nc.vector.drain().then_inc(phase_a, 1)
            dve.wait_ge(phase_a, 4)

            def x1(t):
                return resid[:, bass.ds(t, 1), :, :]

            def x_scales(t, s):
                if isinstance(t, int):
                    dve.wait_ge(x1_s, T)
                after(dve, xa_s, t - 1)
                scales(x1(t).rearrange("p t g e -> p (t g) e"), xam[:, s, :], xsn[:, s, :], xs14[:, s, :],
                       xinv[:, s, :], xam_s, xsn_s, xsc_s, t + 1)

            def h_scales(t, s):
                dve.wait_ge(h_s, 2 * t + 2)
                after(dve, ha_s, t - 1)
                scales(blocks(h[:, s, :]), ham[:, s, :], hsn[:, s, :], hs14[:, s, :], hinv[:, s, :],
                       ham_s, hsn_s, hsc_s, t + 1)

            def x_round(t, s):
                dve.wait_ge(xf_s, t + 1)
                half_up(xq[:, s, :].bitcast(U16), xh_s, xr_s, t + 1)

            def h_round(t, s):
                dve.wait_ge(hf_s, t + 1)
                half_up(hq[:, s, :].bitcast(U16), hh_s, hr_s, t + 1)

            def x_lo(t, s):
                dve.wait_ge(tx_hi, t + 1)
                nc.vector.tensor_tensor(xqT_lo[:, s, :, :], ps[6][:, 0:D].rearrange("p (k n) -> p k n", k=KT),
                                        f32(xqT_hi[:, s, :, :]), ALU.subtract).then_inc(tx_lo, 1)

            def h_lo(t, s):
                for i, (k0, k1, w) in enumerate(((0, 4, 128), (4, 6, 96))):
                    dve.wait_ge(th_hi, 2 * t + i + 1)
                    last = nc.vector.tensor_tensor(
                        hqT_lo[0:w, s, k0:k1, :], ps[4 + i][0:w, 0:(k1 - k0) * P].rearrange("p (k n) -> p k n", n=P),
                        f32(hqT_hi[0:w, s, k0:k1, :]), ALU.subtract)
                last.then_inc(th_lo, 1)

            def gated(t, s, half):
                dve.wait_ge(g_act, 2 * t + half + 1)
                after(dve, hy_s, t - 1)
                nc.vector.tensor_tensor(h[:, s, half * IH:(half + 1) * IH], gact[:, half, :],
                                        ps[2 * half + 1][:, 0:IH], ALU.mult).then_inc(h_s, 1)

            def residual(t, s):
                dve.wait_ge(dn_ps, t + 1)
                nc.vector.tensor_tensor(r3[:, s, :].unsqueeze(1), ps[7][:, 0:D].unsqueeze(1),
                                        x1(t).rearrange("p t g e -> p t (g e)"), ALU.add).then_inc(r3_s, 1)

            def ln3_stats(t, s):
                dve.wait_ge(r3_s, t + 1)
                nc.vector.bn_stats(st3[:, s, :], r3[:, s, :]).then_inc(st3_s, 1)

            def ln3_mean(t, s):
                dve.wait_ge(st3_s, t + 1)
                nc.vector.nop(nofuse=True)
                nc.vector.bn_aggr(mv3[:, s, :], st3[:, s, :]).then_inc(mv3_s, 1)

            def ln3_var(t, s):
                dve.wait_ge(mv3_s, t + 1)
                nc.vector.tensor_scalar(ve3[:, s:s + 1], mv3[:, s, 1:2], EPS_LN, None, ALU.add).then_inc(ve3_s, 1)

            def ln3_apply(t, n):
                s = n % 2
                dve.wait_ge(rstd3_s, t + 1)
                if s == 0:
                    if isinstance(t, int):
                        after(dve, stored[(n // 2) % 2], 16 * (t // 4))
                    else:
                        dve.wait_ge(stored[(n // 2) % 2], (t - n % 4) * 4)
                nc.vector.tensor_scalar(ob[:, (n // 2) % 2, s, :], r3[:, s, :], mv3[:, s, 0:1], rstd3[:, s:s + 1],
                                        ALU.subtract, ALU.mult).then_inc(ob_s, 1)

            def step(t, n, lo=-10, hi=10 ** 9):
                done = lo <= -3
                if done:
                    residual(t - 3, (n + 1) % 2)
                if 0 <= hi:
                    gated(t, n % 2, 0)
                if done:
                    ln3_stats(t - 3, (n + 1) % 2)
                if lo <= -1 and -1 <= hi:
                    h_round(t - 1, (n + 1) % 2)
                if done:
                    ln3_mean(t - 3, (n + 1) % 2)
                if lo <= -2 and -2 <= hi:
                    h_lo(t - 2, n % 2)
                if done:
                    ln3_var(t - 3, (n + 1) % 2)
                if 1 <= hi:
                    x_lo(t + 1, (n + 1) % 2)
                if 2 <= hi:
                    x_scales(t + 2, n % 2)
                if 0 <= hi:
                    gated(t, n % 2, 1)
                    h_scales(t, n % 2)
                if done:
                    ln3_apply(t - 3, n + 1 if not isinstance(t, int) else t - 3)
                if 2 <= hi:
                    x_round(t + 2, n % 2)

            x_scales(0, 0)
            x_scales(1, 1)
            x_round(0, 0)
            x_round(1, 1)
            x_lo(0, 0)
            for n in range(4):
                step(n, n, lo=-n)
            with dve.Fori(1, T // 4 - 1) as i:
                t = i * 4
                for n in range(4):
                    step(t + n, n)
            for n in range(T - 4, T + 3):
                step(n, n, hi=T - 1 - n)

        @block.gpsimd
        def _(pool):
            nc.gpsimd.memset(ident[:, :], 0.0).then_inc(consts_set, 1)
            pool.wait_ge(consts_set, 1)
            nc.gpsimd.affine_select(out=ident[:, :], in_=ident[:, :], compare_op=ALU.not_equal, fill=1.0, base=0,
                                    pattern=[[-1, P]], channel_multiplier=1).then_inc(consts_set, 1)
            pool.wait_ge(small_set, 3)
            pool.wait_ge(consts_set, 2)
            nc.gpsimd.memset(headmask[:, :], 1.0).then_inc(mask_s, 1)
            hm = headmask[:, :].rearrange("p (g e) -> p g e", e=HD)
            pool.wait_ge(mask_s, 1)
            nc.gpsimd.affine_select(out=hm, in_=hm, compare_op=ALU.is_ge, fill=0.0, base=0,
                                    pattern=[[-HD, P // HD], [0, HD]], channel_multiplier=1).then_inc(mask_s, 1)
            pool.wait_ge(mask_s, 2)
            nc.gpsimd.affine_select(out=hm, in_=hm, compare_op=ALU.is_ge, fill=0.0, base=HD - 1,
                                    pattern=[[HD, P // HD], [0, HD]], channel_multiplier=-1).then_inc(consts_set, 2)

            for c, (a, b) in enumerate(CH):
                pool.wait_ge(w_small2, c + 1)
                g = slice(a // BLK, b // BLK)
                nc.gpsimd.tensor_tensor(blocks(wy[:, a:b]), blocks(wraw[:, a:b]), each(winv[:, g]),
                                        ALU.mult).then_inc(w_scaled, 1)
            for c, (a, b) in enumerate(CH):
                pool.wait_ge(w_rounded, c + 1)
                g = slice(a // BLK, b // BLK)
                nc.gpsimd.tensor_tensor(blocks(wa[:, a:b]), blocks(wqn[:, a:b]), each(ws14[:, g]),
                                        ALU.mult).then_inc(w_deq, 1)
            pool.wait_ge(consts_in, 7 * 16)
            pool.wait_ge(watt_lo, 3)
            pool.wait_ge(wT_ps, len(WG))

            def x_bias(t0, hf):
                pool.wait_ge(x_in[hf], t0 * 2 + 16)
                pool.wait_ge(y1_s, t0 + START)
                pool.wait_ge(w1_s, t0 + START)
                nc.gpsimd.tensor_tensor(xbo[:, hf * HALF:(hf + 1) * HALF, :], xin[:, hf * HALF:(hf + 1) * HALF, :],
                                        bo_b[:, :].unsqueeze(1).broadcast_to([P, HALF, D]),
                                        ALU.add).then_inc(x_plus, HALF)

            def k_normalise(t0, r):
                pool.wait_ge(k_norm, t0 + (2 * r + 2))
                pool.wait_ge(kv_acc, t0 + (START + 2 * r - 2) if r >= 2 else t0 + START)
                nc.gpsimd.tensor_tensor(khat[:, r % 2, :, :].rearrange("p j (g e) -> p (j g) e", e=HD),
                                        blocks(kf[:, r % 2, :]), each(knorm[:, r % 2, :]),
                                        ALU.mult).then_inc(k_hat, 2)

            def ln1_affine(t0, r):
                v = t0 + (2 * r + 2)
                pool.wait_ge(z1_s, v)
                nc.gpsimd.tensor_tensor(z1, z1, gamma_b[:, :].unsqueeze(1).broadcast_to([P, 2, D]),
                                        ALU.mult).then_inc(zg_s, 2)
                nc.gpsimd.tensor_tensor(w1[:, r % 2, :, :], xbo[:, 2 * r:2 * r + 2, :],
                                        cb_b[:, :].unsqueeze(1).broadcast_to([P, 2, D]), ALU.add).then_inc(zx_s, 2)
                pool.wait_ge(zg_s, v)
                pool.wait_ge(zx_s, v)
                nc.gpsimd.tensor_tensor(w1[:, r % 2, :, :], w1[:, r % 2, :, :], z1, ALU.add).then_inc(w1_s, 2)

            with pool.Fori(0, B) as b:
                t0 = b * TPB
                x_bias(t0, 0)
                k_normalise(t0, 0)
                k_normalise(t0, 1)
                x_bias(t0, 1)
                k_normalise(t0, 2)
                k_normalise(t0, 3)
                for r in range(NP):
                    ln1_affine(t0, r)

            nc.gpsimd.drain().then_inc(phase_a, 1)
            pool.wait_ge(phase_a, 4)

            def x_scaled(t, s):
                pool.wait_ge(xsc_s, t + 1)
                after(pool, xf_s, t - 1)
                nc.gpsimd.tensor_tensor(blocks(xy[:, s, :]), resid[:, bass.ds(t, 1), :, :].rearrange("p t g e -> p (t g) e"),
                                        each(xinv[:, s, :]), ALU.mult).then_inc(xy_s, 1)

            def x_deq(t, s):
                pool.wait_ge(xr_s, t + 1)
                after(pool, tx_ps, t - 1)
                nc.gpsimd.tensor_tensor(blocks(xa[:, s, :]), blocks(xq[:, s, :].bitcast(F16)), each(xs14[:, s, :]),
                                        ALU.mult).then_inc(xa_s, 1)

            def h_scaled(t, s):
                pool.wait_ge(hsc_s, t + 1)
                after(pool, hf_s, t - 1)
                nc.gpsimd.tensor_tensor(blocks(hy[:, s, :]), blocks(h[:, s, :]), each(hinv[:, s, :]),
                                        ALU.mult).then_inc(hy_s, 1)

            def h_deq(t, s):
                pool.wait_ge(hr_s, t + 1)
                after(pool, th_ps, t - 1)
                nc.gpsimd.tensor_tensor(blocks(ha[:, s, :]), blocks(hq[:, s, :].bitcast(F16)), each(hs14[:, s, :]),
                                        ALU.mult).then_inc(ha_s, 1)

            def ln3_root(t, s):
                pool.wait_ge(ve3_s, t + 1)
                nc.gpsimd.tensor_tensor(rstd3[:, s:s + 1], ve3[:, s:s + 1], mhalf[:, :], ALU.pow).then_inc(rstd3_s, 1)

            def step(t, n, lo=-10, hi=10 ** 9):
                if lo <= -1 and -1 <= hi:
                    h_scaled(t - 1, (n + 1) % 2)
                if 1 <= hi:
                    x_deq(t + 1, (n + 1) % 2)
                if lo <= -1 and -1 <= hi:
                    h_deq(t - 1, (n + 1) % 2)
                if lo <= -3:
                    ln3_root(t - 3, (n + 1) % 2)
                if 2 <= hi:
                    x_scaled(t + 2, n % 2)

            x_scaled(0, 0)
            x_scaled(1, 1)
            x_deq(0, 0)
            for n in range(4):
                step(n, n, lo=-n)
            with pool.Fori(1, T // 4 - 1) as i:
                t = i * 4
                for n in range(4):
                    step(t + n, n)
            for n in range(T - 4, T + 3):
                step(n, n, hi=T - 1 - n)


_INS = ["L0_attn_x", "L0_attn_Wq", "L0_attn_bq", "L0_attn_Wk", "L0_attn_bk", "L0_attn_Wv", "L0_attn_bv", "L0_attn_Wo",
        "L0_attn_bo", "L0_attn_gamma", "L0_attn_beta", "L0_ffn_w_gate", "L0_ffn_w_up", "L0_ffn_w_down"]


def kernel(**inputs):
    import numpy as _np
    import concourse.bacc as _bacc
    from concourse import mybir as _mybir
    from concourse.bass_utils import run_bass_kernel_spmd as _run

    nc = _bacc.Bacc("TRN2", target_bir_lowering=False, num_devices=1)
    arrays, args = {}, []
    for name in _INS:
        a = _np.ascontiguousarray(inputs[name])
        arrays[f"in_{name}_dram"] = a
        args.append(nc.dram_tensor(f"in_{name}_dram", a.shape, _mybir.dt.from_np(a.dtype), kind="ExternalInput").ap())
    shape = inputs["L0_attn_x"].shape
    args.append(nc.dram_tensor("out_dram", shape, _mybir.dt.float32, kind="ExternalOutput").ap())
    build(nc, *args)
    r = _run(nc, [arrays], core_ids=[0])
    return r.results[0]["out_dram"]
```

```python
from contextlib import ExitStack

import concourse.bass as bass
from concourse import mybir

F32 = mybir.dt.float32
F32R = mybir.dt.float32r
F16 = mybir.dt.float16
BF16 = mybir.dt.bfloat16
U16 = mybir.dt.uint16
U32 = mybir.dt.uint32
I32 = mybir.dt.int32
ALU = mybir.AluOpType
ACT = mybir.ActivationFunctionType
AX = mybir.AxisListType

P = 128
BLK = 16
HD = 16
EPS_K = 1e-6
EPS_LN = 1e-5
SCALE_MIN = 1e-12
NUDGE = 1.0 + 2.0 ** -21
F16_ONE = 2.0 ** -14
ROUND_HALF = 0x100
ROUND_MASK = 0xFE00


def after(eng, sem, count):
    if not (isinstance(count, int) and count <= 0):
        eng.wait_ge(sem, count)


def build(nc, x, Wq, bq, Wk, bk, Wv, bv, Wo, bo, gamma, beta, w_gate, w_up, w_down, out):
    B, S, D = x.shape
    I = w_gate.shape[0]
    KT = D // P
    TPB = S // P
    T = B * TPB
    HALF = TPB // 2
    STEPS = 6
    NP = TPB // 2
    IH = I // 2
    VW = D + I
    VB, VC = VW // BLK, 8
    DB, IB = D // BLK, I // BLK
    XC = D // P
    HC = VC - XC
    assert (D, TPB) == (256, 8) and I == 704

    x_rows = x.rearrange("b (p j) d -> (b p) (j d)", j=TPB)
    out_rows = out.rearrange("b (p j) d -> (b p) (j d)", j=TPB)

    with ExitStack() as ctx:
        def sb(name, shape, dt=F32):
            return ctx.enter_context(nc.sbuf_tensor(name, shape, dt))

        def sem(name):
            return ctx.enter_context(nc.semaphore(name))

        resid = sb("resid", [P, T, DB, BLK])
        ident = sb("ident", [P, P])
        actT_hi = sb("actT_hi", [P, 2048], F32R)
        actT_lo = sb("actT_lo", [P, 2048], F32R)
        wkv_hi, wkv_lo = (sb(f"wkv_{n}", [P, KT, 2 * D], F32R) for n in ("hi", "lo"))
        wq_hi, wq_lo = (sb(f"wq_{n}", [P, KT, D], F32R) for n in ("hi", "lo"))
        wo_sb = sb("wo_sb", [P, KT, D])
        wgu_hi, wgu_lo = (sb(f"wgu_{n}", [P, KT, 2 * I], F32R) for n in ("hi", "lo"))
        wd_hi, wd_lo = (sb(f"wd_{n}", [P, HC, D], F32R) for n in ("hi", "lo"))
        headmask = sb("headmask", [P, P])
        rows = sb("rows", [2, 3 * D + P], F32R)
        bq_c = sb("bq_c", [P, KT])
        gamma_b, beta_b = (sb(n, [P, D]) for n in ("gamma_b", "beta_b"))
        mhalf = sb("mhalf", [P, 1])
        mone = sb("mone", [P, 1])
        eps_k = sb("eps_k", [P, 1])

        arena = sb("arena", [P, 18200])
        at = [0]

        def take(words):
            at[0] += words
            assert at[0] <= 18200, at[0]
            return arena[:, at[0] - words:at[0]]

        xin = take(TPB * D).rearrange("p (j d) -> p j d", d=D)
        vb = take(3 * 2 * D).rearrange("p (r j c) -> p r j c", r=3, j=2)
        kexp = take(2 * D).rearrange("p (j c) -> p j c", j=2)
        krelu = take(2 * D).rearrange("p (j c) -> p j c", j=2)
        ksq = take(2 * D)
        kf = take(2 * 2 * D).rearrange("p (s n) -> p s n", s=2)
        khat = take(2 * 2 * D).rearrange("p (s j c) -> p s j c", s=2, j=2)
        kvt = take(KT * P).rearrange("p (m d) -> p m d", m=KT)
        mo = take(KT * D).rearrange("p (m d) -> p m d", m=KT)
        qexp = take(2 * 512).rearrange("p (s n) -> p s n", s=2)
        qrelu = take(2 * 512).rearrange("p (s n) -> p s n", s=2)
        qfT = take(KT * S).rearrange("p (m n) -> p m n", m=KT)
        at_y1 = at[0]
        y1 = take(2 * 2 * D).rearrange("p (s j d) -> p s j d", s=2, j=2)
        z1 = take(2 * D).rearrange("p (j d) -> p j d", j=2)
        w1 = take(2 * 2 * D).rearrange("p (s j d) -> p s j d", s=2, j=2)
        xbeta = take(TPB * D).rearrange("p (j d) -> p j d", d=D)
        ssq, klog, kseed, ku, kv_ = (take(32) for _ in range(5))
        knorm = take(64).rearrange("p (s n) -> p s n", s=2)
        st1, st2 = (take(12).rearrange("p (j n) -> p j n", j=2) for _ in range(2))
        mv1, mv2 = (take(4).rearrange("p (j n) -> p j n", j=2) for _ in range(2))
        ve1, rstd1, nmr1, ve2 = (take(2) for _ in range(4))
        rstd2, nmr2 = (take(4).rearrange("p (s j) -> p s j", s=2) for _ in range(2))
        at[0] = 0
        am, sn, s14, inv = (take(2 * VB).rearrange("p (s n) -> p s n", s=2) for _ in range(4))
        vy = take(2 * VW).rearrange("p (s n) -> p s n", s=2)
        vq = take(VW).rearrange("p (s n) -> p s n", s=2)
        va = take(2 * VC * P).rearrange("p (s n) -> p s n", s=2)
        gact = take(2 * IH).rearrange("p (s n) -> p s n", s=2)
        h = take(2 * I).rearrange("p (s n) -> p s n", s=2)
        r3 = take(2 * D).rearrange("p (s d) -> p s d", s=2)
        ob = take(2 * 2 * D).rearrange("p (s j d) -> p s j d", s=2, j=2)
        st3 = take(12).rearrange("p (s n) -> p s n", s=2)
        mv3 = take(4).rearrange("p (s n) -> p s n", s=2)
        ve3, rstd3, nmean3, nmr3 = (take(2) for _ in range(4))
        scratch = resid[:, :, :, :].rearrange("p t g e -> p (t g e)")
        NW = 2 * I * D // P + D * I // P
        wraw, wy, wa = (scratch[:, i * NW:(i + 1) * NW] for i in range(3))
        wqn = scratch[:, 3 * NW:3 * NW + NW // 2].bitcast(F16)
        o = 3 * NW + NW // 2
        wkv_st = scratch[:, o:o + KT * 2 * D].rearrange("p (k n) -> p k n", k=KT)
        wq_st = scratch[:, o + 1024:o + 1024 + KT * D].rearrange("p (k n) -> p k n", k=KT)
        wsmall = 4 * [None]
        for i in range(4):
            wsmall[i] = arena[:, at_y1 + i * 264:at_y1 + (i + 1) * 264]
        wam, wsn, ws14, winv = wsmall
        rows_st = w1.rearrange("p s j d -> p (s j d)")[0:2, 0:3 * D + P]
        rows_hi = actT_lo[0:2, 0:3 * D + P]

        def halves(y):
            return y.bitcast(BF16).rearrange("p (n two) -> p n two", two=2)[:, :, 1]

        def blocks(a):
            return a.rearrange("p (g e) -> p g e", e=BLK)

        def each(a):
            return a.unsqueeze(2).broadcast_to([P, a.shape[1], BLK])

        xT_hi, xT_lo = (a[:, :].rearrange("p (k n) -> p k n", k=KT) for a in (actT_hi, actT_lo))
        vT_hi, vT_lo = (a[:, :].rearrange("p (s c n) -> p s c n", s=2, c=VC) for a in (actT_hi, actT_lo))

        def f32(a):
            return a.bitcast(F32)

        ps = [ctx.enter_context(nc.psum_tensor(f"bank{i}", [P, 512], F32)) for i in range(8)]

        consts_in, watt_in, wffn_in = sem("consts_in"), sem("watt_in"), sem("wffn_in")
        consts_set, small_set = sem("consts_set"), sem("small_set")
        watt_hi, watt_lo = sem("watt_hi"), sem("watt_lo")
        w_amax, w_nudged, w_scale_s, w_scaled, w_f16, w_half, w_rounded, w_deq, mask_s = (
            sem(n) for n in ("w_amax", "w_nudged", "w_scales", "w_scaled", "w_f16", "w_half", "w_rounded", "w_deq", "mask"))
        wT_ps, wT_hi, wT_lo = sem("wT_ps"), sem("wT_hi"), sem("wT_lo")
        x_in = [sem(f"x_in{i}") for i in range(2)]
        xT_ps, xT_hi_s, xT_lo_s = sem("xT_ps"), sem("xT_hi_done"), sem("xT_lo_done")
        rows_in, rows_st_s, rows_hi_s, rows_lo_s, rows_s = sem("rows_in"), sem("rows_whole"), sem("rows_hi"), sem("rows_lo"), sem("rows_done")
        kv_ps, v_s, k_act, k_feat, k_sq, k_ssq, k_log, k_seed, k_u, k_v, k_norm, k_hat, kv_acc = (
            sem(n) for n in ("kv_ps", "v_copied", "k_act", "k_feat", "k_sq", "k_ssq", "k_log", "k_seed", "k_u",
                             "k_v", "k_norm", "k_hat", "kv_acc"))
        kvt_s, mo_ps, mo_sb = sem("kvt_done"), sem("mo_ps"), sem("mo_sb")
        q_ps, q_act, q_feat = sem("q_ps"), sem("q_act"), sem("q_feat")
        x_plus = sem("x_plus")
        o_ps, y1_s, st1_s, mv1_s, ve1_s, rstd1_s, nmr1_s, z1_s, zg_s, w1_s = (
            sem(n) for n in ("o_ps", "y1_done", "st1_done", "mv1_done", "ve1_done", "rstd1_done", "nmr1_done", "z1_done",
                             "zg_done", "w1_done"))
        st2_s, mv2_s, ve2_s, rstd2_s, nmr2_s, x1_s = (
            sem(n) for n in ("st2_done", "mv2_done", "ve2_done", "rstd2_done", "nmr2_done", "x1_done"))
        phase_a = sem("phase_a")
        am_s, sn_s, scale_s, scaled, f16_s, half_s, round_s, deq_s, pad_s = (
            sem(n) for n in ("amax", "nudged", "scales", "scaled", "f16", "half", "rounded", "dequantised", "pad"))
        vT_ps, vT_hi_s, vT_lo_s = sem("vT_ps"), sem("vT_hi"), sem("vT_lo")
        gu_ps, g_act, h_s = sem("gu_ps"), sem("g_act"), sem("h_done")
        dn_ps, r3_s, st3_s, mv3_s, ve3_s, rstd3_s, nmean3_s, nmr3_s, ob_s = (
            sem(n) for n in ("dn_ps", "r3_done", "st3_done", "mv3_done", "ve3_done", "rstd3_done", "nmean3_done",
                             "nmr3_done", "ob_done"))
        stored = [sem(f"stored{i}") for i in range(2)]

        GU_TILES = 2 * I // P
        DW = KT * I
        CH = [(0, DW), (DW, DW + 6 * D), (DW + 6 * D, NW)]
        WG = []
        for i0, i1 in ((0, 4), (4, 8), (8, GU_TILES)):
            for k in range(KT):
                WG.append(([DW + i * D + k * P for i in range(i0, i1)],
                           wgu_hi[:, k, i0 * P:i1 * P], wgu_lo[:, k, i0 * P:i1 * P]))
        for n in range(KT):
            for k0, k1 in ((0, 4), (4, 6)):
                WG.append(([n * I + k * P for k in range(k0, k1)],
                           wd_hi[:, k0:k1, n * P:(n + 1) * P], wd_lo[:, k0:k1, n * P:(n + 1) * P]))
        W_BANKS = (2, 3, 6, 7)

        def wg_view(g):
            cols, hi, _ = WG[g]
            v = ps[W_BANKS[g % 4]][:, 0:len(cols) * P]
            return v if len(hi.shape) == 2 else v.rearrange("p (k n) -> p k n", n=P)

        def there(t):
            return not isinstance(t, int) or 0 <= t < T

        def joint(n):
            return there(n) or there(n - 3)

        def columns(n):
            return 0 if there(n) else D, VW if there(n - 3) else D

        def chunks(n):
            return 0 if there(n) else XC, VC if there(n - 3) else XC

        def bank_chunks(n):
            c0, c1 = chunks(n)
            return [(ps[4 + a // 4][:, a % 4 * P:(a % 4 + b - a) * P].rearrange("p (k n) -> p k n", n=P), a, b)
                    for a, b in ((c0, min(c1, 4)), (4, c1)) if a < b]

        block = ctx.enter_context(nc.Block())

        @block.sync
        def _(sp):
            for hf in range(2):
                sp.dma_start(xin[:, hf * HALF:(hf + 1) * HALF, :],
                             x_rows[0:P, hf * HALF * D:(hf + 1) * HALF * D]).then_inc(x_in[hf], 16)
            sp.dma_start(wkv_st[:, :, 0:D], Wk.rearrange("(k p) n -> p k n", p=P)).then_inc(watt_in, 16)
            sp.dma_start(wkv_st[:, :, D:2 * D], Wv.rearrange("(k p) n -> p k n", p=P)).then_inc(watt_in, 16)
            sp.dma_start(wq_st, Wq.rearrange("(k p) n -> p k n", p=P)).then_inc(watt_in, 16)
            gu = wraw[:, DW:NW].rearrange("p (i d) -> p i d", d=D)
            whole, part = I // P, I % P
            sp.dma_start(gu[:, 0:whole, :], w_gate[0:whole * P, :].rearrange("(i p) d -> p i d", p=P)).then_inc(wffn_in, 16)
            sp.dma_start(gu[0:part, whole, :], w_gate[whole * P:I, :]).then_inc(wffn_in, 16)
            sp.dma_start(gu[part:P, whole, :], w_up[0:P - part, :]).then_inc(wffn_in, 16)
            sp.dma_start(gu[:, whole + 1:GU_TILES, :],
                         w_up[P - part:I, :].rearrange("(i p) d -> p i d", p=P)).then_inc(wffn_in, 16)
            sp.dma_start(wraw[:, 0:DW].rearrange("p (n c) -> p n c", n=KT),
                         w_down.rearrange("(n p) c -> p n c", p=P)).then_inc(wffn_in, 16)

            with sp.Fori(0, B - 1) as b:
                t0 = b * TPB
                for hf in range(2):
                    sp.wait_ge(xT_ps, t0 + (HALF * (hf + 1)))
                    sp.wait_ge(x_plus, t0 + (HALF * (hf + 1)))
                    sp.dma_start(xin[:, hf * HALF:(hf + 1) * HALF, :],
                                 x_rows[bass.ds(b * P + P, P), hf * HALF * D:(hf + 1) * HALF * D]
                                 ).then_inc(x_in[hf], 16)

            with sp.Fori(0, B) as b:
                t0 = b * TPB
                for r in range(NP):
                    sp.wait_ge(ob_s, t0 + (2 * r + 2))
                    sp.dma_start(out_rows[bass.ds(b * P, P), r * 2 * D:(r + 1) * 2 * D],
                                 ob[:, r % 2, :, :].rearrange("p j d -> p (j d)")).then_inc(stored[r % 2], 16)
            for i in range(2):
                sp.wait_ge(stored[i], 16 * T // 4)

        @block.tensor
        def _(pe):
            def split_product(dst, stat, mov, n, begun=False):
                for k in range(n):
                    (sh, sl), (mh, ml) = stat(k), mov(k)
                    nc.tensor.matmul(dst, sl, mh, start=(k == 0 and not begun), stop=False)
                    nc.tensor.matmul(dst, sh, ml, start=False, stop=False)
                    last = nc.tensor.matmul(dst, sh, mh, start=False, stop=(k == n - 1))
                return last

            def x_transpose(t0, r):
                for j in (2 * r, 2 * r + 1):
                    if j % HALF == 0:
                        pe.wait_ge(x_in[j // HALF], t0 * 2 + 16)
                    after(pe, xT_lo_s, t0 + (j - 1))
                    for k in range(KT):
                        last = nc.tensor.transpose(ps[j % 2][:, k * P:(k + 1) * P], xin[:, j, k * P:(k + 1) * P],
                                                   ident[:, :])
                    last.then_inc(xT_ps, 1)

            def kv_project(t0, r):
                for j in (2 * r, 2 * r + 1):
                    pe.wait_ge(xT_lo_s, t0 + (j + 1))
                    after(pe, k_act, t0 + 2 * r)
                    after(pe, v_s, t0 + 2 * r)
                    c = slice(j * P, (j + 1) * P)
                    nc.tensor.matmul(ps[2 + j % 2][:, :], rows[:, 3 * D:], rows[:, 0:2 * D], start=True, stop=False)
                    split_product(ps[2 + j % 2][:, :], lambda k: (xT_hi[:, k, c], xT_lo[:, k, c]),
                                  lambda k: (wkv_hi[:, k, :], wkv_lo[:, k, :]), KT, begun=True).then_inc(kv_ps, 1)

            def kv_accumulate(t0, r):
                pe.wait_ge(k_hat, t0 + (2 * r + 2))
                if r == 0:
                    after(pe, kvt_s, t0)
                for jj in range(2):
                    j = 2 * r + jj
                    for m in range(KT):
                        last = nc.tensor.matmul(ps[4 + m][:, 0:P], vb[:, r % 3, jj, m * P:(m + 1) * P],
                                                khat[:, r % 2, jj, m * P:(m + 1) * P],
                                                start=(j == 0), stop=(j == TPB - 1))
                    last.then_inc(kv_acc, 1)

            def q_project(t0, g):
                for m in range(KT):
                    u = KT * g + m
                    if u < 2:
                        after(pe, y1_s, t0 + (u - 1))
                    else:
                        pe.wait_ge(q_act, t0 + (2 * (u - 1)))
                    c = slice(g * 512, (g + 1) * 512)
                    split_product(ps[6 + u % 2][:, :],
                                  lambda k: (wq_hi[:, k, m * P:(m + 1) * P], wq_lo[:, k, m * P:(m + 1) * P]),
                                  lambda k: (xT_hi[:, k, c], xT_lo[:, k, c]), KT).then_inc(q_ps, 2)

            def kv_out(t0):
                for m in range(KT):
                    pe.wait_ge(kvt_s, t0 + (4 * (m + 1)))
                    pe.wait_ge(q_act, t0 + (6 + 2 * m))
                    nc.tensor.matmul(ps[6 + m][:, 0:D], kvt[:, m, :], wo_sb[:, m, :],
                                     start=True, stop=True).then_inc(mo_ps, 4)

            def attend(t0, r):
                for j in (2 * r, 2 * r + 1):
                    if j == 0:
                        pe.wait_ge(mo_sb, t0 + TPB)
                    if j % HALF == 0:
                        pe.wait_ge(q_feat, t0 + (HALF * (j // HALF + 1)))
                    if j >= 2:
                        pe.wait_ge(y1_s, t0 + (j - 1))
                    nc.tensor.matmul(ps[6 + j % 2][:, 0:D], rows[:, 3 * D:], rows[:, 2 * D:3 * D], start=True, stop=False)
                    for m in range(KT):
                        last = nc.tensor.matmul(ps[6 + j % 2][:, 0:D], qfT[:, m, j * P:(j + 1) * P], mo[:, m, :],
                                                start=False, stop=(m == KT - 1))
                    last.then_inc(o_ps, 1)

            def batch(t0, new=True, old=True):
                if new:
                    x_transpose(t0, 0)
                    x_transpose(t0, 1)
                for s in range(STEPS):
                    if new and s < NP:
                        kv_project(t0, s)
                    if new and s < 2:
                        x_transpose(t0, s + 2)
                    if old and s < NP:
                        attend(t0 - TPB, s)
                    if new and s >= NP:
                        q_project(t0, s - NP)
                    if new and s >= 2:
                        kv_accumulate(t0, s - 2)
                if new:
                    kv_out(t0)

            pe.wait_ge(consts_set, 2)
            pe.wait_ge(watt_lo, 2)
            pe.wait_ge(rows_s, 2)
            batch(0, old=False)
            pe.wait_ge(w_deq, len(CH))
            pe.wait_ge(k_act, TPB)
            pe.wait_ge(v_s, TPB)
            pe.wait_ge(mo_sb, TPB)
            for g, (cols, _, _) in enumerate(WG):
                after(pe, wT_lo, g - 3)
                for i, c in enumerate(cols):
                    last = nc.tensor.transpose(ps[W_BANKS[g % 4]][:, i * P:(i + 1) * P], wa[:, c:c + P], ident[:, :])
                last.then_inc(wT_ps, 1)
            pe.wait_ge(wT_lo, len(WG))
            with pe.Fori(1, B) as b:
                batch(b * TPB)
            batch(T, new=False)

            nc.tensor.drain().then_inc(phase_a, 1)
            pe.wait_ge(phase_a, 4)

            def gate_up(t, s, half):
                after(pe, h_s, 2 * t + (half - 1))
                for w in range(2):
                    c = slice(w * I + half * IH, w * I + (half + 1) * IH)
                    last = split_product(ps[2 * half + w][:, 0:IH], lambda k: (vT_hi[:, s, k, :], vT_lo[:, s, k, :]),
                                         lambda k: (wgu_hi[:, k, c], wgu_lo[:, k, c]), KT)
                last.then_inc(gu_ps, 1)

            def turn(n, s):
                c0, c1 = chunks(n)
                pe.wait_ge(deq_s, n + 1)
                after(pe, vT_lo_s, n)
                for c in range(c0, c1):
                    last = nc.tensor.transpose(ps[4 + c // 4][:, (c % 4) * P:(c % 4 + 1) * P],
                                               va[:, s, c * P:(c + 1) * P], ident[:, :])
                last.then_inc(vT_ps, 1)

            def down(t, s):
                after(pe, r3_s, t - 1)
                rows = [min(P, I - k * P) for k in range(HC)]
                js = (s + 1) % 2
                split_product(ps[6 + s][:, 0:D],
                              lambda k: (vT_hi[0:rows[k], js, XC + k, :], vT_lo[0:rows[k], js, XC + k, :]),
                              lambda k: (wd_hi[0:rows[k], k, :], wd_lo[0:rows[k], k, :]), HC).then_inc(dn_ps, 1)

            def step(t, n):
                if joint(t):
                    pe.wait_ge(vT_lo_s, t + 1)
                if there(t):
                    gate_up(t, n % 2, 0)
                if joint(t + 1):
                    turn(t + 1, (n + 1) % 2)
                if there(t):
                    gate_up(t, n % 2, 1)
                if there(t - 3):
                    down(t - 3, (n + 1) % 2)

            pe.wait_ge(pad_s, 1)
            turn(0, 0)
            for t in range(8):
                step(t, t % 4)
            with pe.Fori(2, T // 4 - 1) as i:
                for n in range(4):
                    step(i * 4 + n, n)
            for t in range(T - 4, T + 5):
                step(t, t % 4)

        @block.scalar
        def _(act):
            for i, row in enumerate((bk, bv, bo)):
                act.dma_start(rows_st[:, i * D:(i + 1) * D], row.partition_broadcast(2)).then_inc(rows_in, 16)
            act.dma_start(beta_b[:, :], beta.partition_broadcast(P)).then_inc(consts_in, 16)
            act.dma_start(bq_c[:, :], bq.rearrange("(m p) -> p m", p=P), allow_slow_non_contiguous=True).then_inc(consts_in, 16)
            act.dma_start(wo_sb[:, :, :], Wo.rearrange("(k p) n -> p k n", p=P)).then_inc(consts_in, 16)
            act.dma_start(gamma_b[:, :], gamma.partition_broadcast(P)).then_inc(consts_in, 16)
            nc.scalar.preload_act_table_set("natural_log_exp_and_others")
            act.wait_ge(watt_in, 48)
            nc.scalar.activation(wkv_hi[:, :, :], wkv_st, ACT.Copy).then_inc(watt_hi, 1)
            nc.scalar.activation(wq_hi[:, :, :], wq_st, ACT.Copy).then_inc(watt_hi, 1)
            act.wait_ge(rows_st_s, 1)
            nc.scalar.activation(rows_hi, rows_st, ACT.Copy).then_inc(rows_hi_s, 1)
            act.wait_ge(consts_in, 4 * 16)

            def w_f16_chunk(c):
                a, b = CH[c]
                act.wait_ge(w_scaled, c + 1)
                nc.scalar.activation(wqn[:, a:b], halves(wy[:, a:b]), ACT.Copy, scale=F16_ONE).then_inc(w_f16, 1)

            def x_high(t0, r):
                for j in (2 * r, 2 * r + 1):
                    act.wait_ge(xT_ps, t0 + (j + 1))
                    nc.scalar.activation(xT_hi[:, :, j * P:(j + 1) * P],
                                         ps[j % 2][:, 0:D].rearrange("p (k n) -> p k n", k=KT),
                                         ACT.Copy).then_inc(xT_hi_s, 1)

            def k_maps(t0, r):
                for jj in range(2):
                    act.wait_ge(kv_ps, t0 + (2 * r + jj + 1))
                    nc.scalar.activation(kexp[:, jj, :], ps[2 + jj][:, 0:D], ACT.Exp)
                    nc.scalar.activation(krelu[:, jj, :], ps[2 + jj][:, 0:D], ACT.Relu).then_inc(k_act, 1)

            def k_squares(t0, r):
                act.wait_ge(k_feat, t0 + (2 * r + 2))
                nc.scalar.activation(ksq, kf[:, r % 2, :], ACT.Square).then_inc(k_sq, 2)

            def k_seeds(t0, r):
                act.wait_ge(k_ssq, t0 + (2 * r + 2))
                nc.scalar.activation(klog, ssq, ACT.Ln, bias=eps_k[:, :]).then_inc(k_log, 2)
                act.wait_ge(k_log, t0 + (2 * r + 2))
                nc.scalar.activation(kseed, klog, ACT.Exp, scale=-0.5).then_inc(k_seed, 2)

            def q_maps(t0, u):
                act.wait_ge(q_ps, t0 + (2 * (u + 1)))
                after(act, q_feat, t0 + (2 * (u - 1)))
                b = bq_c[:, u % KT:u % KT + 1]
                nc.scalar.activation(qexp[:, u % 2, :], ps[6 + u % 2][:, :], ACT.Exp, bias=b)
                nc.scalar.activation(qrelu[:, u % 2, :], ps[6 + u % 2][:, :], ACT.Relu, bias=b).then_inc(q_act, 2)

            def ln1_apply(t0, r):
                act.wait_ge(nmr1_s, t0 + (2 * r + 2))
                for jj in range(2):
                    last = nc.scalar.activation(z1[:, jj, :], y1[:, r % 2, jj, :], ACT.Identity,
                                                scale=rstd1[:, jj:jj + 1], bias=nmr1[:, jj:jj + 1])
                last.then_inc(z1_s, 2)

            def ln2_apply(t0, r):
                act.wait_ge(nmr2_s, t0 + (2 * r + 2))
                for jj in range(2):
                    nc.scalar.activation(resid[:, bass.ds(t0 + (2 * r + jj), 1), :, :].rearrange("p t g e -> p (t g e)"),
                                         w1[:, r % 2, jj, :], ACT.Identity, scale=rstd2[:, r % 2, jj:jj + 1],
                                         bias=nmr2[:, r % 2, jj:jj + 1]).then_inc(x1_s, 1)

            def batch(t0, new=True, old=True, weights=False):
                u0 = t0 - TPB
                if new:
                    x_high(t0, 0)
                    x_high(t0, 1)
                for s in range(STEPS):
                    if old and 0 <= s - 1 < NP:
                        ln1_apply(u0, s - 1)
                    if new and s < 2:
                        x_high(t0, s + 2)
                    if new and s < NP:
                        k_maps(t0, s)
                    if new and 0 <= s - 1 < NP:
                        k_seeds(t0, s - 1)
                    if new and s < NP:
                        k_squares(t0, s)
                    if new and s >= NP:
                        q_maps(t0, 2 * (s - NP))
                        q_maps(t0, 2 * (s - NP) + 1)
                    if old and s >= 2:
                        ln2_apply(u0, s - 2)
                    if weights and 0 <= s - 1 < len(CH):
                        w_f16_chunk(s - 1)
                if new:
                    for m in range(KT):
                        act.wait_ge(mo_ps, t0 + (4 * (m + 1)))
                        nc.scalar.activation(mo[:, m, :], ps[6 + m][:, 0:D], ACT.Copy).then_inc(mo_sb, 4)

            batch(0, old=False, weights=True)
            for g, (_, hi, _) in enumerate(WG):
                act.wait_ge(wT_ps, g + 1)
                nc.scalar.activation(hi, wg_view(g), ACT.Copy).then_inc(wT_hi, 1)
            with act.Fori(1, B) as b:
                batch(b * TPB)
            batch(T, new=False)

            nc.scalar.drain().then_inc(phase_a, 1)
            nc.scalar.preload_act_table_set("silu_and_others")
            act.wait_ge(phase_a, 4)

            def to_f16(n, s):
                a, b = columns(n)
                act.wait_ge(scaled, n + 1)
                after(act, deq_s, n - 1)
                nc.scalar.activation(vq[:, s, :].bitcast(F16)[:, a:b], halves(vy[:, s, a:b]), ACT.Copy,
                                     scale=F16_ONE).then_inc(f16_s, 1)

            def high(n, s):
                act.wait_ge(vT_ps, n + 1)
                if there(n - 2):
                    after(act, gu_ps, 2 * n - 2)
                after(act, dn_ps, n - 4)
                parts = bank_chunks(n)
                for view, a, b in parts:
                    nc.scalar.activation(vT_hi[:, s, a:b, :], view, ACT.Copy).then_inc(vT_hi_s, 3 - len(parts))

            def silu(t, half):
                act.wait_ge(gu_ps, 2 * t + (half + 1))
                after(act, h_s, 2 * t + (half - 1))
                nc.scalar.activation(gact[:, half, :], ps[2 * half][:, 0:IH], ACT.Silu).then_inc(g_act, 1)

            def ln3_apply(t, n):
                s = n % 2
                act.wait_ge(nmr3_s, t + 1)
                if s == 0:
                    after(act, stored[n // 2], (t - n) * 4)
                nc.scalar.activation(ob[:, n // 2, s, :], r3[:, s, :], ACT.Identity, scale=rstd3[:, s:s + 1],
                                     bias=nmr3[:, s:s + 1]).then_inc(ob_s, 1)

            def step(t, n):
                if there(t):
                    silu(t, 0)
                if there(t - 5):
                    ln3_apply(t - 5, (n + 3) % 4)
                if joint(t + 1):
                    high(t + 1, (n + 1) % 2)
                if joint(t + 2):
                    to_f16(t + 2, n % 2)
                if there(t):
                    silu(t, 1)

            to_f16(0, 0)
            to_f16(1, 1)
            high(0, 0)
            for t in range(8):
                step(t, t % 4)
            with act.Fori(2, T // 4 - 1) as i:
                for n in range(4):
                    step(i * 4 + n, n)
            for t in range(T - 4, T + 5):
                step(t, t % 4)

        @block.vector
        def _(dve):
            nc.vector.memset(mhalf[:, :], -0.5).then_inc(small_set, 1)
            nc.vector.memset(mone[:, :], -1.0).then_inc(small_set, 1)
            nc.vector.memset(eps_k[:, :], EPS_K).then_inc(small_set, 1)
            nc.vector.memset(rows_st[:, 3 * D:], 1.0).then_inc(small_set, 1)
            for i, (lo, hi, st) in enumerate(((wkv_lo, wkv_hi, wkv_st), (wq_lo, wq_hi, wq_st))):
                dve.wait_ge(watt_hi, i + 1)
                nc.vector.tensor_tensor(lo[:, :, :], st, f32(hi[:, :, :]), ALU.subtract).then_inc(watt_lo, 1)
            dve.wait_ge(rows_in, 3 * 16)
            dve.wait_ge(consts_in, 4 * 16)
            dve.wait_ge(small_set, 4)
            nc.vector.tensor_tensor(rows_st[:, 2 * D:3 * D], rows_st[:, 2 * D:3 * D], beta_b[0:2, :],
                                    ALU.subtract).then_inc(rows_st_s, 1)
            dve.wait_ge(rows_hi_s, 1)
            nc.vector.tensor_tensor(rows[:, 0:3 * D], rows_st[:, 0:3 * D], f32(rows_hi[:, 0:3 * D]),
                                    ALU.subtract).then_inc(rows_lo_s, 1)
            nc.vector.tensor_copy(rows[:, 3 * D:], f32(rows_hi[:, 3 * D:])).then_inc(rows_s, 1)
            dve.wait_ge(rows_lo_s, 1)
            nc.vector.tensor_copy(rows[0:1, 0:3 * D], f32(rows_hi[0:1, 0:3 * D])).then_inc(rows_s, 1)

            def scales_of(a, sn_, s14_, inv_, sem_sn, sem_sc, v):
                nc.vector.tensor_scalar(sn_, a, NUDGE / 6.0, SCALE_MIN * NUDGE, ALU.mult, ALU.max).then_inc(sem_sn, 1)
                nc.vector.tensor_scalar(s14_, a, 1.0 / 6.0 / F16_ONE, SCALE_MIN / F16_ONE, ALU.mult, ALU.max)
                dve.wait_ge(sem_sn, v)
                nc.vector.reciprocal(inv_, sn_).then_inc(sem_sc, 1)

            def half_up(q, sem_half, sem_round, v):
                nc.vector.tensor_scalar(q, q, ROUND_HALF, None, ALU.add).then_inc(sem_half, 1)
                dve.wait_ge(sem_half, v)
                nc.vector.tensor_scalar(q, q, ROUND_MASK, None, ALU.bitwise_and).then_inc(sem_round, 1)

            def w_scales(c):
                g = slice(CH[c][0] // BLK, CH[c][1] // BLK)
                dve.wait_ge(wffn_in, 5 * 16)
                nc.vector.tensor_reduce(wam[:, g], blocks(wraw[:, CH[c][0]:CH[c][1]]), AX.X, ALU.max,
                                        apply_absolute_value=True).then_inc(w_amax, 1)
                dve.wait_ge(w_amax, c + 1)
                scales_of(wam[:, g], wsn[:, g], ws14[:, g], winv[:, g], w_nudged, w_scale_s, c + 1)

            def w_round(c):
                dve.wait_ge(w_f16, c + 1)
                half_up(wqn[:, CH[c][0]:CH[c][1]].bitcast(U16), w_half, w_rounded, c + 1)

            def x_low(t0, r):
                for j in (2 * r, 2 * r + 1):
                    c = slice(j * P, (j + 1) * P)
                    dve.wait_ge(xT_hi_s, t0 + (j + 1))
                    nc.vector.tensor_tensor(xT_lo[:, :, c], ps[j % 2][:, 0:D].rearrange("p (k n) -> p k n", k=KT),
                                            f32(xT_hi[:, :, c]), ALU.subtract).then_inc(xT_lo_s, 1)

            def v_copy(t0, r):
                if r == 3:
                    dve.wait_ge(kv_acc, t0 + 2)
                for jj in range(2):
                    dve.wait_ge(k_act, t0 + (2 * r + jj + 1))
                    nc.vector.tensor_copy(vb[:, r % 3, jj, :], ps[2 + jj][:, D:2 * D]).then_inc(v_s, 1)

            def k_features(t0, r):
                dve.wait_ge(k_act, t0 + (2 * r + 2))
                after(dve, k_hat, t0 + (2 * r - 2))
                nc.vector.scalar_tensor_tensor(out=kf[:, r % 2, :], in0=kexp.rearrange("p j c -> p (j c)"), scalar=1.0,
                                               in1=krelu.rearrange("p j c -> p (j c)"), op0=ALU.min,
                                               op1=ALU.add).then_inc(k_feat, 2)

            def k_sums(t0, r):
                dve.wait_ge(k_sq, t0 + (2 * r + 2))
                after(dve, k_norm, t0 + 2 * r)
                nc.vector.tensor_reduce(ssq, ksq.rearrange("p (g e) -> p g e", e=HD), AX.X, ALU.add).then_inc(k_ssq, 2)

            def k_newton(t0, r, part):
                v = t0 + (2 * r + 2)
                if part == 0:
                    dve.wait_ge(k_seed, v)
                    nc.vector.scalar_tensor_tensor(out=ku, in0=ssq, scalar=EPS_K, in1=kseed, op0=ALU.add,
                                                   op1=ALU.mult).then_inc(k_u, 2)
                elif part == 1:
                    dve.wait_ge(k_u, v)
                    nc.vector.scalar_tensor_tensor(out=kv_, in0=ku, scalar=-0.5, in1=kseed, op0=ALU.mult,
                                                   op1=ALU.mult).then_inc(k_v, 2)
                else:
                    dve.wait_ge(k_v, v)
                    nc.vector.scalar_tensor_tensor(out=knorm[:, r % 2, :], in0=kv_, scalar=1.5, in1=kseed, op0=ALU.add,
                                                   op1=ALU.mult).then_inc(k_norm, 2)

            def q_features(t0, u):
                dve.wait_ge(q_act, t0 + (2 * (u + 1)))
                nc.vector.scalar_tensor_tensor(out=qfT[:, u % KT, (u // KT) * 512:(u // KT + 1) * 512],
                                               in0=qexp[:, u % 2, :], scalar=1.0, in1=qrelu[:, u % 2, :],
                                               op0=ALU.min, op1=ALU.add).then_inc(q_feat, 2)

            def ln1_sum(t0, r):
                for jj in range(2):
                    j = 2 * r + jj
                    dve.wait_ge(o_ps, t0 + (j + 1))
                    if jj == 0:
                        dve.wait_ge(x_plus, t0 + (2 * r + 2))
                    nc.vector.tensor_tensor(y1[:, r % 2, jj, :], ps[6 + j % 2][:, 0:D], xbeta[:, j, :],
                                            ALU.add).then_inc(y1_s, 1)

            def ln_stats(t0, r, y, st, s_y, s_st):
                dve.wait_ge(s_y, t0 + (2 * r + 2))
                for jj in range(2):
                    nc.vector.bn_stats(st[:, jj, :], y[:, r % 2, jj, :]).then_inc(s_st, 1)

            def ln_means(t0, r, st, mv, s_st, s_mv):
                dve.wait_ge(s_st, t0 + (2 * r + 2))
                nc.vector.nop(nofuse=True)
                for jj in range(2):
                    nc.vector.bn_aggr(mv[:, jj, :], st[:, jj, :]).then_inc(s_mv, 1)

            def add_eps(t0, r, mv, eps, ve, s_mv, s_ve):
                dve.wait_ge(s_mv, t0 + (2 * r + 2))
                nc.vector.tensor_scalar(ve, mv[:, :, 1], eps, None, ALU.add).then_inc(s_ve, 2)

            def shift(t0, r, mv, rstd, nmr, s_rstd, s_nmr):
                dve.wait_ge(s_rstd, t0 + (2 * r + 2))
                nc.vector.scalar_tensor_tensor(out=nmr, in0=mv[:, :, 0], scalar=-1.0, in1=rstd, op0=ALU.mult,
                                               op1=ALU.mult).then_inc(s_nmr, 2)

            def batch(t0, new=True, old=True, weights=False):
                u0 = t0 - TPB
                if new:
                    x_low(t0, 0)
                    x_low(t0, 1)
                for s in range(STEPS):
                    ln1, ln2, newton = old and s < NP, old and s >= 2, new and 0 <= s - 1 < NP
                    if old and 0 <= s - 1 < NP:
                        shift(u0, s - 1, mv1, rstd1, nmr1, rstd1_s, nmr1_s)
                    if new and 0 <= s - 1 < NP:
                        k_sums(t0, s - 1)
                    if ln2:
                        ln_stats(u0, s - 2, w1, st2, w1_s, st2_s)
                    if new and s < 2:
                        x_low(t0, s + 2)
                    if new and s < NP:
                        v_copy(t0, s)
                    if ln2:
                        ln_means(u0, s - 2, st2, mv2, st2_s, mv2_s)
                    if new and s < NP:
                        k_features(t0, s)
                    if newton:
                        k_newton(t0, s - 1, 0)
                    if ln2:
                        add_eps(u0, s - 2, mv2, EPS_LN, ve2, mv2_s, ve2_s)
                    if ln1:
                        ln1_sum(u0, s)
                    if newton:
                        k_newton(t0, s - 1, 1)
                    if ln1:
                        ln_stats(u0, s, y1, st1, y1_s, st1_s)
                    if newton:
                        k_newton(t0, s - 1, 2)
                    if ln1:
                        ln_means(u0, s, st1, mv1, st1_s, mv1_s)
                    if ln2:
                        shift(u0, s - 2, mv2, rstd2[:, s % 2, :], nmr2[:, s % 2, :], rstd2_s, nmr2_s)
                    if ln1:
                        add_eps(u0, s, mv1, EPS_K, ve1, mv1_s, ve1_s)
                    if new and s >= NP:
                        q_features(t0, 2 * (s - NP))
                        q_features(t0, 2 * (s - NP) + 1)
                    if weights and s < len(CH):
                        w_scales(s)
                    if weights and 0 <= s - 2 < len(CH):
                        w_round(s - 2)
                if new:
                    dve.wait_ge(kv_acc, t0 + TPB)
                    for m in range(KT):
                        nc.vector.tensor_tensor(kvt[:, m, :], ps[4 + m][:, 0:P], headmask[:, :],
                                                ALU.mult).then_inc(kvt_s, 4)

            dve.wait_ge(consts_set, 4)
            batch(0, old=False, weights=True)
            for g, (_, hi, lo) in enumerate(WG):
                dve.wait_ge(wT_hi, g + 1)
                nc.vector.tensor_tensor(lo, wg_view(g), f32(hi), ALU.subtract).then_inc(wT_lo, 1)
            with dve.Fori(1, B) as b:
                batch(b * TPB)
            batch(T, new=False)

            nc.vector.drain().then_inc(phase_a, 1)
            dve.wait_ge(phase_a, 4)

            nc.vector.memset(va[:, :, VW:VC * P], 0.0).then_inc(pad_s, 1)

            def x1(t):
                return resid[:, bass.ds(t, 1), :, :]

            def amax_x(n, s):
                after(dve, deq_s, n - 1)
                nc.vector.tensor_reduce(am[:, s, 0:DB], x1(n).rearrange("p t g e -> p (t g) e"), AX.X, ALU.max,
                                        apply_absolute_value=True).then_inc(am_s, 1 if there(n - 3) else 2)

            def amax_h(n, s):
                after(dve, deq_s, n - 1)
                dve.wait_ge(h_s, 2 * n - 4)
                nc.vector.tensor_reduce(am[:, s, DB:VB], blocks(h[:, 1 - s, :]), AX.X, ALU.max,
                                        apply_absolute_value=True).then_inc(am_s, 1 if there(n) else 2)

            def joint_scales(n, s):
                a, b = (c // BLK for c in columns(n))
                dve.wait_ge(am_s, 2 * n + 2)
                scales_of(am[:, s, a:b], sn[:, s, a:b], s14[:, s, a:b], inv[:, s, a:b], sn_s, scale_s, n + 1)

            def round_off(n, s):
                a, b = columns(n)
                dve.wait_ge(f16_s, n + 1)
                half_up(vq[:, s, :].bitcast(U16)[:, a:b], half_s, round_s, n + 1)

            def low(n, s):
                parts = bank_chunks(n)
                for i, (view, a, b) in enumerate(parts):
                    dve.wait_ge(vT_hi_s, 2 * n + 1 + i)
                    last = nc.vector.tensor_tensor(vT_lo[:, s, a:b, :], view, f32(vT_hi[:, s, a:b, :]), ALU.subtract)
                last.then_inc(vT_lo_s, 1)

            def gated(t, s, half):
                dve.wait_ge(g_act, 2 * t + (half + 1))
                if half == 0:
                    after(dve, scaled, t + 2 if not isinstance(t, int) or t >= 2 else 0)
                nc.vector.tensor_tensor(h[:, s, half * IH:(half + 1) * IH], gact[:, half, :],
                                        ps[2 * half + 1][:, 0:IH], ALU.mult).then_inc(h_s, 1)

            def residual(t, s):
                dve.wait_ge(dn_ps, t + 1)
                after(dve, ob_s, t - 1)
                nc.vector.tensor_tensor(r3[:, s, :].unsqueeze(1), ps[6 + s][:, 0:D].unsqueeze(1),
                                        x1(t).rearrange("p t g e -> p t (g e)"), ALU.add).then_inc(r3_s, 1)

            def ln3_stats(t, s):
                dve.wait_ge(r3_s, t + 1)
                nc.vector.bn_stats(st3[:, s, :], r3[:, s, :]).then_inc(st3_s, 1)

            def ln3_mean(t, s):
                dve.wait_ge(st3_s, t + 1)
                nc.vector.nop(nofuse=True)
                nc.vector.bn_aggr(mv3[:, s, :], st3[:, s, :]).then_inc(mv3_s, 1)

            def ln3_var(t, s):
                dve.wait_ge(mv3_s, t + 1)
                nc.vector.tensor_scalar(ve3[:, s:s + 1], mv3[:, s, 1:2], EPS_LN, None, ALU.add).then_inc(ve3_s, 1)

            def step(t, n):
                s, o = n % 2, (n + 1) % 2
                done = there(t - 4)
                if done:
                    residual(t - 4, s)
                if there(t):
                    gated(t, s, 0)
                if done:
                    ln3_stats(t - 4, s)
                if joint(t + 1):
                    low(t + 1, o)
                if done:
                    ln3_mean(t - 4, s)
                if joint(t + 2):
                    round_off(t + 2, s)
                if done:
                    ln3_var(t - 4, s)
                if there(t + 3):
                    amax_x(t + 3, o)
                if there(t):
                    gated(t, s, 1)
                    amax_h(t + 3, o)
                if joint(t + 3):
                    joint_scales(t + 3, o)

            amax_x(0, 0)
            joint_scales(0, 0)
            amax_x(1, 1)
            joint_scales(1, 1)
            round_off(0, 0)
            round_off(1, 1)
            amax_x(2, 0)
            joint_scales(2, 0)
            low(0, 0)
            for t in range(8):
                step(t, t % 4)
            with dve.Fori(2, T // 4 - 1) as i:
                for n in range(4):
                    step(i * 4 + n, n)
            for t in range(T - 4, T + 5):
                step(t, t % 4)

        @block.gpsimd
        def _(pool):
            nc.gpsimd.memset(ident[:, :], 0.0).then_inc(consts_set, 1)
            pool.wait_ge(consts_set, 1)
            nc.gpsimd.affine_select(out=ident[:, :], in_=ident[:, :], compare_op=ALU.not_equal, fill=1.0, base=0,
                                    pattern=[[-1, P]], channel_multiplier=1).then_inc(consts_set, 1)
            pool.wait_ge(consts_set, 2)
            nc.gpsimd.memset(headmask[:, :], 1.0).then_inc(mask_s, 1)
            hm = headmask[:, :].rearrange("p (g e) -> p g e", e=HD)
            pool.wait_ge(mask_s, 1)
            nc.gpsimd.affine_select(out=hm, in_=hm, compare_op=ALU.is_ge, fill=0.0, base=0,
                                    pattern=[[-HD, P // HD], [0, HD]], channel_multiplier=1).then_inc(mask_s, 1)
            pool.wait_ge(mask_s, 2)
            nc.gpsimd.affine_select(out=hm, in_=hm, compare_op=ALU.is_ge, fill=0.0, base=HD - 1,
                                    pattern=[[HD, P // HD], [0, HD]], channel_multiplier=-1).then_inc(consts_set, 2)
            pool.wait_ge(small_set, 4)
            pool.wait_ge(consts_in, 4 * 16)

            def w_scaled_chunk(c):
                a, b = CH[c]
                pool.wait_ge(w_scale_s, c + 1)
                nc.gpsimd.tensor_tensor(blocks(wy[:, a:b]), blocks(wraw[:, a:b]), each(winv[:, a // BLK:b // BLK]),
                                        ALU.mult).then_inc(w_scaled, 1)

            def w_deq_chunk(c):
                a, b = CH[c]
                pool.wait_ge(w_rounded, c + 1)
                nc.gpsimd.tensor_tensor(blocks(wa[:, a:b]), blocks(wqn[:, a:b]), each(ws14[:, a // BLK:b // BLK]),
                                        ALU.mult).then_inc(w_deq, 1)

            def x_bias(t0, r):
                if r % 2 == 0:
                    pool.wait_ge(x_in[r // 2], t0 * 2 + 16)
                after(pool, w1_s, t0 - TPB + (2 * r + 2))
                nc.gpsimd.tensor_tensor(xbeta[:, 2 * r:2 * r + 2, :], xin[:, 2 * r:2 * r + 2, :],
                                        beta_b[:, :].unsqueeze(1).broadcast_to([P, 2, D]),
                                        ALU.add).then_inc(x_plus, 2)

            def k_normalise(t0, r):
                pool.wait_ge(k_norm, t0 + (2 * r + 2))
                after(pool, kv_acc, t0 + (2 * r - 2))
                nc.gpsimd.tensor_tensor(khat[:, r % 2, :, :].rearrange("p j (g e) -> p (j g) e", e=HD),
                                        blocks(kf[:, r % 2, :]), each(knorm[:, r % 2, :]),
                                        ALU.mult).then_inc(k_hat, 2)

            def ln1_affine(t0, r):
                v = t0 + (2 * r + 2)
                pool.wait_ge(z1_s, v)
                nc.gpsimd.tensor_tensor(z1, z1, gamma_b[:, :].unsqueeze(1).broadcast_to([P, 2, D]),
                                        ALU.mult).then_inc(zg_s, 2)
                pool.wait_ge(zg_s, v)
                nc.gpsimd.tensor_tensor(w1[:, r % 2, :, :], z1, xbeta[:, 2 * r:2 * r + 2, :], ALU.add).then_inc(w1_s, 2)

            def root(t0, r, ve, rstd, s_ve, s_rstd):
                pool.wait_ge(s_ve, t0 + (2 * r + 2))
                nc.gpsimd.tensor_tensor(rstd, ve, mhalf[:, :].broadcast_to([P, 2]), ALU.pow).then_inc(s_rstd, 2)

            def batch(t0, new=True, old=True, weights=False):
                u0 = t0 - TPB
                for s in range(STEPS):
                    if old and 0 <= s - 1 < NP:
                        ln1_affine(u0, s - 1)
                    if old and s >= 2:
                        root(u0, s - 2, ve2, rstd2[:, s % 2, :], ve2_s, rstd2_s)
                    if new and 0 <= s - 1 < NP:
                        k_normalise(t0, s - 1)
                    if old and s < NP:
                        root(u0, s, ve1, rstd1, ve1_s, rstd1_s)
                    if new and 0 <= s - 1 < NP:
                        x_bias(t0, s - 1)
                    if weights and 0 <= s - 1 < len(CH):
                        w_scaled_chunk(s - 1)
                    if weights and 0 <= s - 2 < len(CH):
                        w_deq_chunk(s - 2)

            batch(0, old=False, weights=True)
            with pool.Fori(1, B) as b:
                batch(b * TPB)
            batch(T, new=False)

            nc.gpsimd.drain().then_inc(phase_a, 1)
            pool.wait_ge(phase_a, 4)

            def over_scales(n, s):
                pool.wait_ge(scale_s, n + 1)
                after(pool, f16_s, n - 1)
                if there(n - 3):
                    last = nc.gpsimd.tensor_tensor(blocks(vy[:, s, D:VW]), blocks(h[:, 1 - s, :]), each(inv[:, s, DB:VB]),
                                                   ALU.mult)
                if there(n):
                    last = nc.gpsimd.tensor_tensor(blocks(vy[:, s, 0:D]),
                                                   resid[:, bass.ds(n, 1), :, :].rearrange("p t g e -> p (t g) e"),
                                                   each(inv[:, s, 0:DB]), ALU.mult)
                last.then_inc(scaled, 1)

            def dequantise(n, s):
                a, b = columns(n)
                pool.wait_ge(round_s, n + 1)
                after(pool, vT_ps, n - 1)
                nc.gpsimd.tensor_tensor(blocks(va[:, s, a:b]), blocks(vq[:, s, :].bitcast(F16)[:, a:b]),
                                        each(s14[:, s, a // BLK:b // BLK]), ALU.mult).then_inc(deq_s, 1)

            def ln3_root(t, s):
                pool.wait_ge(ve3_s, t + 1)
                nc.gpsimd.tensor_tensor(rstd3[:, s:s + 1], ve3[:, s:s + 1], mhalf[:, :], ALU.pow).then_inc(rstd3_s, 1)
                nc.gpsimd.tensor_tensor(nmean3[:, s:s + 1], mv3[:, s, 0:1], mone[:, :], ALU.mult).then_inc(nmean3_s, 1)
                pool.wait_ge(rstd3_s, t + 1)
                pool.wait_ge(nmean3_s, t + 1)
                nc.gpsimd.tensor_tensor(nmr3[:, s:s + 1], nmean3[:, s:s + 1], rstd3[:, s:s + 1],
                                        ALU.mult).then_inc(nmr3_s, 1)

            def step(t, n):
                if joint(t + 2):
                    over_scales(t + 2, n % 2)
                    dequantise(t + 2, n % 2)
                if there(t - 4):
                    ln3_root(t - 4, n % 2)

            for n in range(2):
                over_scales(n, n)
            for n in range(2):
                dequantise(n, n)
            for t in range(8):
                step(t, t % 4)
            with pool.Fori(2, T // 4 - 1) as i:
                for n in range(4):
                    step(i * 4 + n, n)
            for t in range(T - 4, T + 5):
                step(t, t % 4)


_INS = ["L0_attn_x", "L0_attn_Wq", "L0_attn_bq", "L0_attn_Wk", "L0_attn_bk", "L0_attn_Wv", "L0_attn_bv", "L0_attn_Wo",
        "L0_attn_bo", "L0_attn_gamma", "L0_attn_beta", "L0_ffn_w_gate", "L0_ffn_w_up", "L0_ffn_w_down"]


def kernel(**inputs):
    import numpy as _np
    import concourse.bacc as _bacc
    from concourse import mybir as _mybir
    from concourse.bass_utils import run_bass_kernel_spmd as _run

    nc = _bacc.Bacc("TRN2", target_bir_lowering=False, num_devices=1)
    arrays, args = {}, []
    for name in _INS:
        a = _np.ascontiguousarray(inputs[name])
        arrays[f"in_{name}_dram"] = a
        args.append(nc.dram_tensor(f"in_{name}_dram", a.shape, _mybir.dt.from_np(a.dtype), kind="ExternalInput").ap())
    shape = inputs["L0_attn_x"].shape
    args.append(nc.dram_tensor("out_dram", shape, _mybir.dt.float32, kind="ExternalOutput").ap())
    build(nc, *args)
    r = _run(nc, [arrays], core_ids=[0])
    return r.results[0]["out_dram"]
```

```python
from contextlib import ExitStack

import concourse.bass as bass
from concourse import mybir

F32 = mybir.dt.float32
F32R = mybir.dt.float32r
F16 = mybir.dt.float16
BF16 = mybir.dt.bfloat16
U16 = mybir.dt.uint16
U32 = mybir.dt.uint32
I32 = mybir.dt.int32
ALU = mybir.AluOpType
ACT = mybir.ActivationFunctionType
AX = mybir.AxisListType

P = 128
BLK = 16
HD = 16
EPS_K = 1e-6
EPS_LN = 1e-5
SCALE_MIN = 1e-12
NUDGE = 1.0 + 2.0 ** -21
F16_ONE = 2.0 ** -14
ROUND_HALF = 0x100
ROUND_MASK = 0xFE00


def after(eng, sem, count):
    if not (isinstance(count, int) and count <= 0):
        eng.wait_ge(sem, count)


def build(nc, x, Wq, bq, Wk, bk, Wv, bv, Wo, bo, gamma, beta, w_gate, w_up, w_down, out):
    B, S, D = x.shape
    I = w_gate.shape[0]
    KT = D // P
    TPB = S // P
    T = B * TPB
    LAG = 4
    STEPS = 6
    NP = TPB // 2
    IH = I // 2
    VW = D + I
    VB, VC = VW // BLK, 8
    DB, IB = D // BLK, I // BLK
    XC = D // P
    HC = VC - XC
    assert (D, TPB) == (256, 8) and I == 704

    x_rows = x.rearrange("b (p j) d -> (b p) (j d)", j=TPB)
    out_rows = out.rearrange("b (p j) d -> (b p) (j d)", j=TPB)

    with ExitStack() as ctx:
        def sb(name, shape, dt=F32):
            return ctx.enter_context(nc.sbuf_tensor(name, shape, dt))

        def sem(name):
            return ctx.enter_context(nc.semaphore(name))

        resid = sb("resid", [P, T, DB, BLK])
        ident = sb("ident", [P, P])
        actT_hi = sb("actT_hi", [P, 2048], F32R)
        actT_lo = sb("actT_lo", [P, 2048], F32R)
        wkv_hi, wkv_lo = (sb(f"wkv_{n}", [P, KT, 2 * D], F32R) for n in ("hi", "lo"))
        wq_hi, wq_lo = (sb(f"wq_{n}", [P, KT, D], F32R) for n in ("hi", "lo"))
        wo_sb = sb("wo_sb", [P, KT, D])
        wgu_hi, wgu_lo = (sb(f"wgu_{n}", [P, KT, 2 * I], F32R) for n in ("hi", "lo"))
        wd_hi, wd_lo = (sb(f"wd_{n}", [P, HC, D], F32R) for n in ("hi", "lo"))
        headmask = sb("headmask", [P, P])
        rows_hi = sb("rows_hi", [2, 3 * D + P], F32R)
        rows = sb("rows", [2, 3 * D + P], F32R)
        bq_c = sb("bq_c", [P, KT])
        gamma_b, beta_b = (sb(n, [P, D]) for n in ("gamma_b", "beta_b"))
        mhalf = sb("mhalf", [P, 1])
        mone = sb("mone", [P, 1])
        eps_k = sb("eps_k", [P, 1])

        ARENA = 16960
        arena = sb("arena", [P, ARENA])
        at = [0]

        def take(words):
            at[0] += words
            assert at[0] <= ARENA, at[0]
            return arena[:, at[0] - words:at[0]]

        xin = take(TPB * D).rearrange("p (j d) -> p j d", d=D)
        vb = take(3 * 2 * D).rearrange("p (r j c) -> p r j c", r=3, j=2)
        kexp = take(2 * D).rearrange("p (j c) -> p j c", j=2)
        krelu = take(2 * D).rearrange("p (j c) -> p j c", j=2)
        ksq = take(2 * D)
        kf = take(2 * 2 * D).rearrange("p (s n) -> p s n", s=2)
        khat = take(2 * 2 * D).rearrange("p (s j c) -> p s j c", s=2, j=2)
        kvt = take(KT * P).rearrange("p (m d) -> p m d", m=KT)
        qexp = take(2 * 512).rearrange("p (s n) -> p s n", s=2)
        qrelu = take(2 * 512).rearrange("p (s n) -> p s n", s=2)
        ssq, klog, kseed, ku, kv_ = (take(32) for _ in range(5))
        knorm = take(64).rearrange("p (s n) -> p s n", s=2)
        kept_from = at[0]
        qfT = take(KT * S).rearrange("p (m n) -> p m n", m=KT)
        mo = take(KT * D).rearrange("p (m d) -> p m d", m=KT)
        at_y1 = at[0]
        y1 = take(2 * 2 * D).rearrange("p (s j d) -> p s j d", s=2, j=2)
        z1 = take(2 * D).rearrange("p (j d) -> p j d", j=2)
        w1 = take(2 * 2 * D).rearrange("p (s j d) -> p s j d", s=2, j=2)
        xbeta = take(TPB * D).rearrange("p (j d) -> p j d", d=D)
        st1, st2 = (take(12).rearrange("p (j n) -> p j n", j=2) for _ in range(2))
        mv1 = take(4).rearrange("p (j n) -> p j n", j=2)
        mv2 = take(8).rearrange("p (s j n) -> p s j n", s=2, j=2)
        ve1, rstd1, nmr1 = (take(2) for _ in range(3))
        ve2, rstd2, nmr2 = (take(4).rearrange("p (s j) -> p s j", s=2) for _ in range(3))
        at[0] = 0
        am, sn, s14, inv = (take(2 * VB).rearrange("p (s n) -> p s n", s=2) for _ in range(4))
        vy = take(2 * VW).rearrange("p (s n) -> p s n", s=2)
        vq = take(VW).rearrange("p (s n) -> p s n", s=2)
        va = take(2 * VC * P).rearrange("p (s n) -> p s n", s=2)
        gact = take(2 * IH).rearrange("p (s n) -> p s n", s=2)
        h = take(2 * I).rearrange("p (s n) -> p s n", s=2)
        r3 = take(2 * D).rearrange("p (s d) -> p s d", s=2)
        ob = take(2 * 2 * D).rearrange("p (s j d) -> p s j d", s=2, j=2)
        st3 = take(12).rearrange("p (s n) -> p s n", s=2)
        mv3 = take(4).rearrange("p (s n) -> p s n", s=2)
        ve3, rstd3, nmean3, nmr3 = (take(2) for _ in range(4))
        assert at[0] <= kept_from
        scratch = resid[:, :, :, :].rearrange("p t g e -> p (t g e)")
        NW = 2 * I * D // P + D * I // P
        wraw, wy, wa = (scratch[:, i * NW:(i + 1) * NW] for i in range(3))
        wqn = scratch[:, 3 * NW:3 * NW + NW // 2].bitcast(F16)
        o = 3 * NW + NW // 2
        wkv_st = scratch[:, o:o + KT * 2 * D].rearrange("p (k n) -> p k n", k=KT)
        wq_st = scratch[:, o + 1024:o + 1024 + KT * D].rearrange("p (k n) -> p k n", k=KT)
        NB = NW // BLK
        wam, wsn, ws14, winv = (arena[:, at_y1 + i * NB:at_y1 + (i + 1) * NB] for i in range(4))
        rows_st = w1.rearrange("p s j d -> p (s j d)")[0:2, 0:3 * D + P]

        def halves(y):
            return y.bitcast(BF16).rearrange("p (n two) -> p n two", two=2)[:, :, 1]

        def blocks(a):
            return a.rearrange("p (g e) -> p g e", e=BLK)

        def each(a):
            return a.unsqueeze(2).broadcast_to([P, a.shape[1], BLK])

        xT_hi, xT_lo = (a[:, :].rearrange("p (k n) -> p k n", k=KT) for a in (actT_hi, actT_lo))
        vT_hi, vT_lo = (a[:, :].rearrange("p (s c n) -> p s c n", s=2, c=VC) for a in (actT_hi, actT_lo))

        def f32(a):
            return a.bitcast(F32)

        ps = [ctx.enter_context(nc.psum_tensor(f"bank{i}", [P, 512], F32)) for i in range(8)]

        consts_in, watt_in, wffn_in = sem("consts_in"), sem("watt_in"), sem("wffn_in")
        consts_set, small_set = sem("consts_set"), sem("small_set")
        watt_hi, watt_lo = sem("watt_hi"), sem("watt_lo")
        w_amax, w_nudged, w_scale_s, w_scaled, w_f16, w_half, w_rounded, w_deq, mask_s = (
            sem(n) for n in ("w_amax", "w_nudged", "w_scales", "w_scaled", "w_f16", "w_half", "w_rounded", "w_deq", "mask"))
        wT_ps, wT_hi, wT_lo = sem("wT_ps"), sem("wT_hi"), sem("wT_lo")
        x_in = [sem(f"x_in{i}") for i in range(NP)]
        xT_ps, xT_hi_s, xT_lo_s = sem("xT_ps"), sem("xT_hi_done"), sem("xT_lo_done")
        rows_in, rows_st_s, rows_hi_s, rows_lo_s, rows_s = sem("rows_in"), sem("rows_whole"), sem("rows_hi"), sem("rows_lo"), sem("rows_done")
        kv_ps, v_s, k_act, k_feat, k_sq, k_ssq, k_log, k_seed, k_u, k_v, k_norm, k_hat, kv_acc = (
            sem(n) for n in ("kv_ps", "v_copied", "k_act", "k_feat", "k_sq", "k_ssq", "k_log", "k_seed", "k_u",
                             "k_v", "k_norm", "k_hat", "kv_acc"))
        kvt_s, mo_ps, mo_sb = sem("kvt_done"), sem("mo_ps"), sem("mo_sb")
        q_ps, q_act, q_feat = sem("q_ps"), sem("q_act"), sem("q_feat")
        x_plus = sem("x_plus")
        o_ps, y1_s, st1_s, mv1_s, ve1_s, rstd1_s, nmr1_s, z1_s, zg_s, w1_s = (
            sem(n) for n in ("o_ps", "y1_done", "st1_done", "mv1_done", "ve1_done", "rstd1_done", "nmr1_done", "z1_done",
                             "zg_done", "w1_done"))
        st2_s, mv2_s, ve2_s, rstd2_s, nmr2_s, x1_s = (
            sem(n) for n in ("st2_done", "mv2_done", "ve2_done", "rstd2_done", "nmr2_done", "x1_done"))
        phase_a = sem("phase_a")
        am_s, sn_s, scale_s, scaled, f16_s, half_s, round_s, deq_s, pad_s = (
            sem(n) for n in ("amax", "nudged", "scales", "scaled", "f16", "half", "rounded", "dequantised", "pad"))
        vT_ps, vT_hi_s, vT_lo_s = sem("vT_ps"), sem("vT_hi"), sem("vT_lo")
        gu_ps, g_act, h_s = sem("gu_ps"), sem("g_act"), sem("h_done")
        dn_ps, r3_s, st3_s, mv3_s, ve3_s, rstd3_s, nmean3_s, nmr3_s, ob_s = (
            sem(n) for n in ("dn_ps", "r3_done", "st3_done", "mv3_done", "ve3_done", "rstd3_done", "nmean3_done",
                             "nmr3_done", "ob_done"))
        stored = [sem(f"stored{i}") for i in range(2)]

        GU_TILES = 2 * I // P
        DW = KT * I
        CH = [(0, DW), (DW, DW + 6 * D), (DW + 6 * D, NW)]
        WG = []
        for n in range(KT):
            for k0, k1 in ((0, 4), (4, 6)):
                WG.append((1 if n == 0 or k1 == 4 else 2, [n * I + k * P for k in range(k0, k1)],
                           wd_hi[:, k0:k1, n * P:(n + 1) * P], wd_lo[:, k0:k1, n * P:(n + 1) * P]))
        for i0, i1 in ((0, 4), (4, 8), (8, GU_TILES)):
            for k in range(KT):
                WG.append((2 if i1 <= 6 else 3, [DW + i * D + k * P for i in range(i0, i1)],
                           wgu_hi[:, k, i0 * P:i1 * P], wgu_lo[:, k, i0 * P:i1 * P]))
        W_BANKS = (2, 3, 6, 7)

        def wg_view(g):
            _, cols, hi, _ = WG[g]
            v = ps[W_BANKS[g % 4]][:, 0:len(cols) * P]
            return v if len(hi.shape) == 2 else v.rearrange("p (k n) -> p k n", n=P)

        def there(t):
            return not isinstance(t, int) or 0 <= t < T

        def joint(n):
            return there(n) or there(n - LAG)

        def columns(n):
            return 0 if there(n) else D, VW if there(n - LAG) else D

        def chunks(n):
            return 0 if there(n) else XC, VC if there(n - LAG) else XC

        def bank_chunks(n):
            c0, c1 = chunks(n)
            return [(ps[4 + a // 4][:, a % 4 * P:(a % 4 + b - a) * P].rearrange("p (k n) -> p k n", n=P), a, b)
                    for a, b in ((c0, min(c1, 4)), (4, c1)) if a < b]

        block = ctx.enter_context(nc.Block())

        @block.sync
        def _(sp):
            for r in range(NP):
                sp.dma_start(xin[:, 2 * r:2 * r + 2, :], x_rows[0:P, 2 * r * D:(2 * r + 2) * D]).then_inc(x_in[r], 16)
            sp.dma_start(wkv_st[:, :, 0:D], Wk.rearrange("(k p) n -> p k n", p=P)).then_inc(watt_in, 16)
            sp.dma_start(wkv_st[:, :, D:2 * D], Wv.rearrange("(k p) n -> p k n", p=P)).then_inc(watt_in, 16)
            sp.dma_start(wq_st, Wq.rearrange("(k p) n -> p k n", p=P)).then_inc(watt_in, 16)
            gu = wraw[:, DW:NW].rearrange("p (i d) -> p i d", d=D)
            whole, part = I // P, I % P
            sp.dma_start(gu[:, 0:whole, :], w_gate[0:whole * P, :].rearrange("(i p) d -> p i d", p=P)).then_inc(wffn_in, 16)
            sp.dma_start(gu[0:part, whole, :], w_gate[whole * P:I, :]).then_inc(wffn_in, 16)
            sp.dma_start(gu[part:P, whole, :], w_up[0:P - part, :]).then_inc(wffn_in, 16)
            sp.dma_start(gu[:, whole + 1:GU_TILES, :],
                         w_up[P - part:I, :].rearrange("(i p) d -> p i d", p=P)).then_inc(wffn_in, 16)
            sp.dma_start(wraw[:, 0:DW].rearrange("p (n c) -> p n c", n=KT),
                         w_down.rearrange("(n p) c -> p n c", p=P)).then_inc(wffn_in, 16)

            with sp.Fori(0, B - 1) as b:
                t0 = b * TPB
                for r in range(NP):
                    sp.wait_ge(xT_ps, t0 + (2 * r + 2))
                    sp.wait_ge(x_plus, t0 + (2 * r + 2))
                    sp.dma_start(xin[:, 2 * r:2 * r + 2, :],
                                 x_rows[bass.ds(b * P + P, P), 2 * r * D:(2 * r + 2) * D]).then_inc(x_in[r], 16)

            with sp.Fori(0, B) as b:
                t0 = b * TPB
                for r in range(NP):
                    sp.wait_ge(ob_s, t0 + (2 * r + 2))
                    sp.dma_start(out_rows[bass.ds(b * P, P), r * 2 * D:(r + 1) * 2 * D],
                                 ob[:, r % 2, :, :].rearrange("p j d -> p (j d)")).then_inc(stored[r % 2], 16)
            for i in range(2):
                sp.wait_ge(stored[i], 16 * T // 4)

        @block.tensor
        def _(pe):
            def split_product(dst, stat, mov, n, begun=False):
                for k in range(n):
                    (sh, sl), (mh, ml) = stat(k), mov(k)
                    nc.tensor.matmul(dst, sl, mh, start=(k == 0 and not begun), stop=False)
                    nc.tensor.matmul(dst, sh, ml, start=False, stop=False)
                    last = nc.tensor.matmul(dst, sh, mh, start=False, stop=(k == n - 1))
                return last

            def x_transpose(t0, r):
                for j in (2 * r, 2 * r + 1):
                    if j % 2 == 0:
                        pe.wait_ge(x_in[r], t0 * 2 + 16)
                    after(pe, xT_lo_s, t0 + (j - 1))
                    for k in range(KT):
                        last = nc.tensor.transpose(ps[j % 2][:, k * P:(k + 1) * P], xin[:, j, k * P:(k + 1) * P],
                                                   ident[:, :])
                    last.then_inc(xT_ps, 1)

            def kv_project(t0, r):
                for j in (2 * r, 2 * r + 1):
                    pe.wait_ge(xT_lo_s, t0 + (j + 1))
                    after(pe, k_act, t0 + 2 * r)
                    after(pe, v_s, t0 + 2 * r)
                    c = slice(j * P, (j + 1) * P)
                    nc.tensor.matmul(ps[2 + j % 2][:, :], rows[:, 3 * D:], rows[:, 0:2 * D], start=True, stop=False)
                    split_product(ps[2 + j % 2][:, :], lambda k: (xT_hi[:, k, c], xT_lo[:, k, c]),
                                  lambda k: (wkv_hi[:, k, :], wkv_lo[:, k, :]), KT, begun=True).then_inc(kv_ps, 1)

            def kv_accumulate(t0, r):
                pe.wait_ge(k_hat, t0 + (2 * r + 2))
                if r == 0:
                    after(pe, kvt_s, t0)
                for jj in range(2):
                    j = 2 * r + jj
                    for m in range(KT):
                        last = nc.tensor.matmul(ps[4 + m][:, 0:P], vb[:, r % 3, jj, m * P:(m + 1) * P],
                                                khat[:, r % 2, jj, m * P:(m + 1) * P],
                                                start=(j == 0), stop=(j == TPB - 1))
                    last.then_inc(kv_acc, 1)

            def q_project(t0, g):
                for m in range(KT):
                    u = KT * g + m
                    if u < 2:
                        after(pe, y1_s, t0 + (u - 1))
                    else:
                        pe.wait_ge(q_act, t0 + (2 * (u - 1)))
                    c = slice(g * 512, (g + 1) * 512)
                    split_product(ps[6 + u % 2][:, :],
                                  lambda k: (wq_hi[:, k, m * P:(m + 1) * P], wq_lo[:, k, m * P:(m + 1) * P]),
                                  lambda k: (xT_hi[:, k, c], xT_lo[:, k, c]), KT).then_inc(q_ps, 2)

            def kv_out(t0):
                for m in range(KT):
                    pe.wait_ge(kvt_s, t0 + (4 * (m + 1)))
                    pe.wait_ge(q_act, t0 + (6 + 2 * m))
                    nc.tensor.matmul(ps[6 + m][:, 0:D], kvt[:, m, :], wo_sb[:, m, :],
                                     start=True, stop=True).then_inc(mo_ps, 4)

            def attend(t0, r):
                for j in (2 * r, 2 * r + 1):
                    if j == 0:
                        pe.wait_ge(mo_sb, t0 + TPB)
                    if j % 4 == 0:
                        pe.wait_ge(q_feat, t0 + (j + 4))
                    if j >= 2:
                        pe.wait_ge(y1_s, t0 + (j - 1))
                    nc.tensor.matmul(ps[6 + j % 2][:, 0:D], rows[:, 3 * D:], rows[:, 2 * D:3 * D], start=True, stop=False)
                    for m in range(KT):
                        last = nc.tensor.matmul(ps[6 + j % 2][:, 0:D], qfT[:, m, j * P:(j + 1) * P], mo[:, m, :],
                                                start=False, stop=(m == KT - 1))
                    last.then_inc(o_ps, 1)

            def batch(t0, new=True, old=True, more=True):
                for s in range(STEPS):
                    if new and s < NP:
                        kv_project(t0, s)
                    if new and s < 2:
                        x_transpose(t0, s + 2)
                    if old and s < NP:
                        attend(t0 - TPB, s)
                    if new and s >= NP:
                        q_project(t0, s - NP)
                    if new and s >= 2:
                        kv_accumulate(t0, s - 2)
                if more:
                    x_transpose(t0 + TPB, 0)
                if new:
                    kv_out(t0)
                if more:
                    x_transpose(t0 + TPB, 1)

            pe.wait_ge(consts_set, 2)
            x_transpose(0, 0)
            x_transpose(0, 1)
            pe.wait_ge(watt_lo, 2)
            pe.wait_ge(rows_s, 2)
            batch(0, old=False)
            pe.wait_ge(k_act, TPB)
            pe.wait_ge(v_s, TPB)
            pe.wait_ge(mo_sb, TPB)
            for g, (chunks_in, cols, _, _) in enumerate(WG):
                pe.wait_ge(w_deq, chunks_in)
                after(pe, wT_lo, g - 3)
                for i, c in enumerate(cols):
                    last = nc.tensor.transpose(ps[W_BANKS[g % 4]][:, i * P:(i + 1) * P], wa[:, c:c + P], ident[:, :])
                last.then_inc(wT_ps, 1)
            pe.wait_ge(wT_lo, len(WG))
            with pe.Fori(1, B - 1) as b:
                batch(b * TPB)
            batch(T - TPB, more=False)
            nc.tensor.drain().then_inc(phase_a, 1)
            batch(T, new=False, more=False)
            pe.wait_ge(phase_a, 4)

            def gate_up(t, s, half):
                after(pe, h_s, 2 * t + (half - 1))
                for w in range(2):
                    c = slice(w * I + half * IH, w * I + (half + 1) * IH)
                    last = split_product(ps[2 * half + w][:, 0:IH], lambda k: (vT_hi[:, s, k, :], vT_lo[:, s, k, :]),
                                         lambda k: (wgu_hi[:, k, c], wgu_lo[:, k, c]), KT)
                last.then_inc(gu_ps, 1)

            def turn(n, s):
                c0, c1 = chunks(n)
                pe.wait_ge(deq_s, n + 1)
                after(pe, vT_lo_s, n)
                for c in range(c0, c1):
                    last = nc.tensor.transpose(ps[4 + c // 4][:, (c % 4) * P:(c % 4 + 1) * P],
                                               va[:, s, c * P:(c + 1) * P], ident[:, :])
                last.then_inc(vT_ps, 1)

            def down(t, s):
                after(pe, r3_s, t - 1)
                rows = [min(P, I - k * P) for k in range(HC)]
                split_product(ps[6 + s][:, 0:D],
                              lambda k: (vT_hi[0:rows[k], s, XC + k, :], vT_lo[0:rows[k], s, XC + k, :]),
                              lambda k: (wd_hi[0:rows[k], k, :], wd_lo[0:rows[k], k, :]), HC).then_inc(dn_ps, 1)

            def step(t, n):
                if joint(t):
                    pe.wait_ge(vT_lo_s, t + 1)
                if there(t):
                    gate_up(t, n % 2, 0)
                if joint(t + 1):
                    turn(t + 1, (n + 1) % 2)
                if there(t):
                    gate_up(t, n % 2, 1)
                if there(t - LAG):
                    down(t - LAG, n % 2)

            pe.wait_ge(pad_s, 1)
            turn(0, 0)
            for t in range(12):
                step(t, t % 4)
            with pe.Fori(3, T // 4 - 1) as i:
                for n in range(4):
                    step(i * 4 + n, n)
            for t in range(T - 4, T + 6):
                step(t, t % 4)

        @block.scalar
        def _(act):
            for i, row in enumerate((bk, bv, bo)):
                act.dma_start(rows_st[:, i * D:(i + 1) * D], row.partition_broadcast(2)).then_inc(rows_in, 16)
            act.dma_start(beta_b[:, :], beta.partition_broadcast(P)).then_inc(rows_in, 16)
            act.dma_start(bq_c[:, :], bq.rearrange("(m p) -> p m", p=P), allow_slow_non_contiguous=True).then_inc(consts_in, 16)
            act.dma_start(wo_sb[:, :, :], Wo.rearrange("(k p) n -> p k n", p=P)).then_inc(consts_in, 16)
            act.dma_start(gamma_b[:, :], gamma.partition_broadcast(P)).then_inc(consts_in, 16)
            nc.scalar.preload_act_table_set("natural_log_exp_and_others")

            def first_highs():
                x_high(0, 0)
                act.wait_ge(rows_st_s, 1)
                nc.scalar.activation(rows_hi[:, :], rows_st, ACT.Copy).then_inc(rows_hi_s, 1)
                x_high(0, 1)
                act.wait_ge(watt_in, 48)
                nc.scalar.activation(wkv_hi[:, :, :], wkv_st, ACT.Copy).then_inc(watt_hi, 1)
                nc.scalar.activation(wq_hi[:, :, :], wq_st, ACT.Copy).then_inc(watt_hi, 1)
                act.wait_ge(consts_in, 3 * 16)

            def w_f16_chunk(c):
                a, b = CH[c]
                act.wait_ge(w_scaled, c + 1)
                nc.scalar.activation(wqn[:, a:b], halves(wy[:, a:b]), ACT.Copy, scale=F16_ONE).then_inc(w_f16, 1)

            def x_high(t0, r):
                for j in (2 * r, 2 * r + 1):
                    act.wait_ge(xT_ps, t0 + (j + 1))
                    nc.scalar.activation(xT_hi[:, :, j * P:(j + 1) * P],
                                         ps[j % 2][:, 0:D].rearrange("p (k n) -> p k n", k=KT),
                                         ACT.Copy).then_inc(xT_hi_s, 1)

            def k_maps(t0, r, jj):
                act.wait_ge(kv_ps, t0 + (2 * r + jj + 1))
                nc.scalar.activation(kexp[:, jj, :], ps[2 + jj][:, 0:D], ACT.Exp)
                nc.scalar.activation(krelu[:, jj, :], ps[2 + jj][:, 0:D], ACT.Relu).then_inc(k_act, 1)

            def k_squares(t0, r):
                act.wait_ge(k_feat, t0 + (2 * r + 2))
                nc.scalar.activation(ksq, kf[:, r % 2, :], ACT.Square).then_inc(k_sq, 2)

            def k_seeds(t0, r):
                act.wait_ge(k_ssq, t0 + (2 * r + 2))
                nc.scalar.activation(klog, ssq, ACT.Ln, bias=eps_k[:, :]).then_inc(k_log, 2)
                act.wait_ge(k_log, t0 + (2 * r + 2))
                nc.scalar.activation(kseed, klog, ACT.Exp, scale=-0.5).then_inc(k_seed, 2)

            def q_maps(t0, u):
                act.wait_ge(q_ps, t0 + (2 * (u + 1)))
                after(act, q_feat, t0 + (2 * (u - 1)))
                b = bq_c[:, u % KT:u % KT + 1]
                nc.scalar.activation(qexp[:, u % 2, :], ps[6 + u % 2][:, :], ACT.Exp, bias=b)
                nc.scalar.activation(qrelu[:, u % 2, :], ps[6 + u % 2][:, :], ACT.Relu, bias=b).then_inc(q_act, 2)

            def ln1_apply(t0, r):
                act.wait_ge(nmr1_s, t0 + (2 * r + 2))
                for jj in range(2):
                    last = nc.scalar.activation(z1[:, jj, :], y1[:, r % 2, jj, :], ACT.Identity,
                                                scale=rstd1[:, jj:jj + 1], bias=nmr1[:, jj:jj + 1])
                last.then_inc(z1_s, 2)

            def ln2_apply(t0, r):
                act.wait_ge(nmr2_s, t0 + (2 * r + 2))
                for jj in range(2):
                    nc.scalar.activation(resid[:, bass.ds(t0 + (2 * r + jj), 1), :, :].rearrange("p t g e -> p (t g e)"),
                                         w1[:, r % 2, jj, :], ACT.Identity, scale=rstd2[:, r % 2, jj:jj + 1],
                                         bias=nmr2[:, r % 2, jj:jj + 1]).then_inc(x1_s, 1)

            def batch(t0, new=True, old=True, more=True, weights=False):
                u0 = t0 - TPB
                for s in range(STEPS):
                    if new and s < NP:
                        k_maps(t0, s, 0)
                        k_maps(t0, s, 1)
                    if new and 0 <= s - 1 < NP:
                        k_seeds(t0, s - 1)
                    if new and s < 2:
                        x_high(t0, s + 2)
                    if new and s >= NP:
                        q_maps(t0, 2 * (s - NP))
                        q_maps(t0, 2 * (s - NP) + 1)
                    if more and s == STEPS - 1:
                        x_high(t0 + TPB, 0)
                    if old and 3 <= s < STEPS - 1:
                        ln2_apply(u0, s - 3)
                    if old and 0 <= s - 1 < NP:
                        ln1_apply(u0, s - 1)
                    if new and s < NP:
                        k_squares(t0, s)
                    if not new:
                        begin(s)
                    if weights and 0 <= s - 2 < len(CH):
                        w_f16_chunk(s - 2)
                if new:
                    for m in range(KT):
                        act.wait_ge(mo_ps, t0 + (4 * (m + 1)))
                        nc.scalar.activation(mo[:, m, :], ps[6 + m][:, 0:D], ACT.Copy).then_inc(mo_sb, 4)
                if more:
                    x_high(t0 + TPB, 1)
                if old and new:
                    ln2_apply(u0, 2)
                    ln2_apply(u0, 3)

            first_highs()
            batch(0, old=False, weights=True)
            for g, (_, _, hi, _) in enumerate(WG):
                act.wait_ge(wT_ps, g + 1)
                nc.scalar.activation(hi, wg_view(g), ACT.Copy).then_inc(wT_hi, 1)
            with act.Fori(1, B - 1) as b:
                batch(b * TPB)
            batch(T - TPB, more=False)
            nc.scalar.drain().then_inc(phase_a, 1)
            nc.scalar.preload_act_table_set("silu_and_others")

            def to_f16(n, s):
                a, b = columns(n)
                act.wait_ge(scaled, n + 1)
                after(act, deq_s, n - 1)
                nc.scalar.activation(vq[:, s, :].bitcast(F16)[:, a:b], halves(vy[:, s, a:b]), ACT.Copy,
                                     scale=F16_ONE).then_inc(f16_s, 1)

            def high(n, s):
                act.wait_ge(vT_ps, n + 1)
                if there(n - 2):
                    after(act, gu_ps, 2 * n - 2)
                after(act, dn_ps, n - (LAG + 1))
                parts = bank_chunks(n)
                for view, a, b in parts:
                    nc.scalar.activation(vT_hi[:, s, a:b, :], view, ACT.Copy).then_inc(vT_hi_s, 3 - len(parts))

            def silu(t, half):
                act.wait_ge(gu_ps, 2 * t + (half + 1))
                after(act, h_s, 2 * t + (half - 1))
                nc.scalar.activation(gact[:, half, :], ps[2 * half][:, 0:IH], ACT.Silu).then_inc(g_act, 1)

            def ln3_apply(t, n):
                s = n % 2
                act.wait_ge(nmr3_s, t + 1)
                if s == 0:
                    after(act, stored[n // 2], (t - n) * 4)
                nc.scalar.activation(ob[:, n // 2, s, :], r3[:, s, :], ACT.Identity, scale=rstd3[:, s:s + 1],
                                     bias=nmr3[:, s:s + 1]).then_inc(ob_s, 1)

            def step(t, n):
                if there(t):
                    silu(t, 0)
                if joint(t + 1):
                    high(t + 1, (n + 1) % 2)
                if there(t):
                    silu(t, 1)
                if joint(t + 3):
                    to_f16(t + 3, (n + 1) % 2)
                if there(t - 6):
                    ln3_apply(t - 6, (n + 2) % 4)

            def begin(s):
                if s == 1:
                    act.wait_ge(phase_a, 4)
                    to_f16(0, 0)
                elif s == 2:
                    to_f16(1, 1)
                elif s == 3:
                    high(0, 0)
                elif s == 4:
                    to_f16(2, 0)

            batch(T, new=False, more=False)
            for t in range(12):
                step(t, t % 4)
                if t in (0, 2):
                    ln2_apply(T - TPB, 2 + t // 2)
            with act.Fori(3, T // 4 - 1) as i:
                for n in range(4):
                    step(i * 4 + n, n)
            for t in range(T - 4, T + 6):
                step(t, t % 4)

        @block.vector
        def _(dve):
            nc.vector.memset(mhalf[:, :], -0.5).then_inc(small_set, 1)
            nc.vector.memset(mone[:, :], -1.0).then_inc(small_set, 1)
            nc.vector.memset(eps_k[:, :], EPS_K).then_inc(small_set, 1)
            nc.vector.memset(rows_st[:, 3 * D:], 1.0).then_inc(small_set, 1)

            def first_lows():
                dve.wait_ge(rows_in, 4 * 16)
                dve.wait_ge(small_set, 4)
                nc.vector.tensor_tensor(rows_st[:, 2 * D:3 * D], rows_st[:, 2 * D:3 * D], beta_b[0:2, :],
                                        ALU.subtract).then_inc(rows_st_s, 1)
                x_low(0, 0)
                dve.wait_ge(rows_hi_s, 1)
                nc.vector.tensor_tensor(rows[:, 0:3 * D], rows_st[:, 0:3 * D], f32(rows_hi[:, 0:3 * D]),
                                        ALU.subtract).then_inc(rows_lo_s, 1)
                nc.vector.tensor_copy(rows[:, 3 * D:], f32(rows_hi[:, 3 * D:])).then_inc(rows_s, 1)
                dve.wait_ge(rows_lo_s, 1)
                nc.vector.tensor_copy(rows[0:1, 0:3 * D], f32(rows_hi[0:1, 0:3 * D])).then_inc(rows_s, 1)
                x_low(0, 1)
                for i, (lo, hi, st) in enumerate(((wkv_lo, wkv_hi, wkv_st), (wq_lo, wq_hi, wq_st))):
                    dve.wait_ge(watt_hi, i + 1)
                    nc.vector.tensor_tensor(lo[:, :, :], st, f32(hi[:, :, :]), ALU.subtract).then_inc(watt_lo, 1)

            def scales_of(a, sn_, s14_, inv_, sem_sn, sem_sc, v):
                nc.vector.tensor_scalar(sn_, a, NUDGE / 6.0, SCALE_MIN * NUDGE, ALU.mult, ALU.max).then_inc(sem_sn, 1)
                nc.vector.tensor_scalar(s14_, a, 1.0 / 6.0 / F16_ONE, SCALE_MIN / F16_ONE, ALU.mult, ALU.max)
                dve.wait_ge(sem_sn, v)
                nc.vector.reciprocal(inv_, sn_).then_inc(sem_sc, 1)

            def half_up(q, sem_half, sem_round, v):
                nc.vector.tensor_scalar(q, q, ROUND_HALF, None, ALU.add).then_inc(sem_half, 1)
                dve.wait_ge(sem_half, v)
                nc.vector.tensor_scalar(q, q, ROUND_MASK, None, ALU.bitwise_and).then_inc(sem_round, 1)

            def w_scales(c):
                g = slice(CH[c][0] // BLK, CH[c][1] // BLK)
                dve.wait_ge(wffn_in, 5 * 16)
                nc.vector.tensor_reduce(wam[:, g], blocks(wraw[:, CH[c][0]:CH[c][1]]), AX.X, ALU.max,
                                        apply_absolute_value=True).then_inc(w_amax, 1)
                dve.wait_ge(w_amax, c + 1)
                scales_of(wam[:, g], wsn[:, g], ws14[:, g], winv[:, g], w_nudged, w_scale_s, c + 1)

            def w_round(c):
                dve.wait_ge(w_f16, c + 1)
                half_up(wqn[:, CH[c][0]:CH[c][1]].bitcast(U16), w_half, w_rounded, c + 1)

            def x_low(t0, r):
                for j in (2 * r, 2 * r + 1):
                    c = slice(j * P, (j + 1) * P)
                    dve.wait_ge(xT_hi_s, t0 + (j + 1))
                    nc.vector.tensor_tensor(xT_lo[:, :, c], ps[j % 2][:, 0:D].rearrange("p (k n) -> p k n", k=KT),
                                            f32(xT_hi[:, :, c]), ALU.subtract).then_inc(xT_lo_s, 1)

            def v_copy(t0, r, jj):
                if r == 3:
                    dve.wait_ge(kv_acc, t0 + 2)
                dve.wait_ge(k_act, t0 + (2 * r + jj + 1))
                nc.vector.tensor_copy(vb[:, r % 3, jj, :], ps[2 + jj][:, D:2 * D]).then_inc(v_s, 1)

            def k_features(t0, r):
                dve.wait_ge(k_act, t0 + (2 * r + 2))
                after(dve, k_hat, t0 + (2 * r - 2))
                nc.vector.scalar_tensor_tensor(out=kf[:, r % 2, :], in0=kexp.rearrange("p j c -> p (j c)"), scalar=1.0,
                                               in1=krelu.rearrange("p j c -> p (j c)"), op0=ALU.min,
                                               op1=ALU.add).then_inc(k_feat, 2)

            def k_sums(t0, r):
                dve.wait_ge(k_sq, t0 + (2 * r + 2))
                after(dve, k_norm, t0 + 2 * r)
                nc.vector.tensor_reduce(ssq, ksq.rearrange("p (g e) -> p g e", e=HD), AX.X, ALU.add).then_inc(k_ssq, 2)

            def k_newton(t0, r, part):
                v = t0 + (2 * r + 2)
                if part == 0:
                    dve.wait_ge(k_seed, v)
                    nc.vector.scalar_tensor_tensor(out=ku, in0=ssq, scalar=EPS_K, in1=kseed, op0=ALU.add,
                                                   op1=ALU.mult).then_inc(k_u, 2)
                elif part == 1:
                    dve.wait_ge(k_u, v)
                    nc.vector.scalar_tensor_tensor(out=kv_, in0=ku, scalar=-0.5, in1=kseed, op0=ALU.mult,
                                                   op1=ALU.mult).then_inc(k_v, 2)
                else:
                    dve.wait_ge(k_v, v)
                    nc.vector.scalar_tensor_tensor(out=knorm[:, r % 2, :], in0=kv_, scalar=1.5, in1=kseed, op0=ALU.add,
                                                   op1=ALU.mult).then_inc(k_norm, 2)

            def q_features(t0, u):
                dve.wait_ge(q_act, t0 + (2 * (u + 1)))
                nc.vector.scalar_tensor_tensor(out=qfT[:, u % KT, (u // KT) * 512:(u // KT + 1) * 512],
                                               in0=qexp[:, u % 2, :], scalar=1.0, in1=qrelu[:, u % 2, :],
                                               op0=ALU.min, op1=ALU.add).then_inc(q_feat, 2)

            def ln1_sum(t0, r):
                if r == 3:
                    dve.wait_ge(z1_s, t0 + 4)
                for jj in range(2):
                    j = 2 * r + jj
                    dve.wait_ge(o_ps, t0 + (j + 1))
                    if jj == 0:
                        dve.wait_ge(x_plus, t0 + (2 * r + 2))
                    nc.vector.tensor_tensor(y1[:, r % 2, jj, :], ps[6 + j % 2][:, 0:D], xbeta[:, j, :],
                                            ALU.add).then_inc(y1_s, 1)

            def ln_stats(t0, r, y, st, s_y, s_st):
                dve.wait_ge(s_y, t0 + (2 * r + 2))
                for jj in range(2):
                    nc.vector.bn_stats(st[:, jj, :], y[:, r % 2, jj, :]).then_inc(s_st, 1)

            def ln_means(t0, r, st, mv, s_st, s_mv):
                dve.wait_ge(s_st, t0 + (2 * r + 2))
                nc.vector.nop(nofuse=True)
                for jj in range(2):
                    nc.vector.bn_aggr(mv[:, jj, :], st[:, jj, :]).then_inc(s_mv, 1)

            def add_eps(t0, r, mv, eps, ve, s_mv, s_ve):
                dve.wait_ge(s_mv, t0 + (2 * r + 2))
                nc.vector.tensor_scalar(ve, mv[:, :, 1], eps, None, ALU.add).then_inc(s_ve, 2)

            def shift(t0, r, mv, rstd, nmr, s_rstd, s_nmr):
                dve.wait_ge(s_rstd, t0 + (2 * r + 2))
                nc.vector.scalar_tensor_tensor(out=nmr, in0=mv[:, :, 0], scalar=-1.0, in1=rstd, op0=ALU.mult,
                                               op1=ALU.mult).then_inc(s_nmr, 2)

            def ln2_shift(t0, r):
                shift(t0, r, mv2[:, r % 2, :, :], rstd2[:, r % 2, :], nmr2[:, r % 2, :], rstd2_s, nmr2_s)

            def ln2_variance(t0, r):
                ln_stats(t0, r, w1, st2, w1_s, st2_s)
                ln_means(t0, r, st2, mv2[:, r % 2, :, :], st2_s, mv2_s)
                add_eps(t0, r, mv2[:, r % 2, :, :], EPS_LN, ve2[:, r % 2, :], mv2_s, ve2_s)

            def batch(t0, new=True, old=True, more=True, weights=False):
                u0 = t0 - TPB
                for s in range(STEPS):
                    ln1, ln2, newton = old and s < NP, old and 2 <= s < STEPS - 1, new and 0 <= s - 1 < NP
                    if newton:
                        k_sums(t0, s - 1)
                    if new and s < NP:
                        v_copy(t0, s, 0)
                        v_copy(t0, s, 1)
                    if old and 0 < s < 3:
                        shift(u0, s - 1, mv1, rstd1, nmr1, rstd1_s, nmr1_s)
                    if new and s < NP:
                        k_features(t0, s)
                    if newton:
                        k_newton(t0, s - 1, 0)
                    if ln1 and s == 3:
                        ln1_sum(u0, s)
                    if old and s == 3:
                        shift(u0, s - 1, mv1, rstd1, nmr1, rstd1_s, nmr1_s)
                        ln2_shift(u0, s - 3)
                    if ln2:
                        ln_stats(u0, s - 2, w1, st2, w1_s, st2_s)
                    if new and s < 2:
                        x_low(t0, s + 2)
                    if ln1 and s != 3:
                        ln1_sum(u0, s)
                    if newton:
                        k_newton(t0, s - 1, 1)
                    if ln2:
                        ln_means(u0, s - 2, st2, mv2[:, s % 2, :, :], st2_s, mv2_s)
                    if ln1:
                        ln_stats(u0, s, y1, st1, y1_s, st1_s)
                    if newton:
                        k_newton(t0, s - 1, 2)
                    if ln1:
                        ln_means(u0, s, st1, mv1, st1_s, mv1_s)
                    if old and s == NP:
                        ln2_shift(u0, s - 3)
                    if ln2:
                        add_eps(u0, s - 2, mv2[:, s % 2, :, :], EPS_LN, ve2[:, s % 2, :], mv2_s, ve2_s)
                    if ln1:
                        add_eps(u0, s, mv1, EPS_K, ve1, mv1_s, ve1_s)
                    if old and s == NP:
                        shift(u0, s - 1, mv1, rstd1, nmr1, rstd1_s, nmr1_s)
                    if new and s == STEPS - 1:
                        dve.wait_ge(kv_acc, t0 + TPB)
                        for m in range(KT):
                            nc.vector.tensor_tensor(kvt[:, m, :], ps[4 + m][:, 0:P], headmask[:, :],
                                                    ALU.mult).then_inc(kvt_s, 4)
                    if new and s >= NP:
                        q_features(t0, 2 * (s - NP))
                        q_features(t0, 2 * (s - NP) + 1)
                    if not new:
                        begin(s)
                    if weights and s < len(CH):
                        w_scales(s)
                    if weights and 0 <= s - 3 < len(CH):
                        w_round(s - 3)
                if more:
                    x_low(t0 + TPB, 0)
                if old:
                    ln2_shift(u0, 2)
                if old and new:
                    ln2_variance(u0, 3)
                if more:
                    x_low(t0 + TPB, 1)
                if old and new:
                    ln2_shift(u0, 3)

            first_lows()
            dve.wait_ge(consts_set, 4)
            batch(0, old=False, weights=True)
            for g, (_, _, hi, lo) in enumerate(WG):
                dve.wait_ge(wT_hi, g + 1)
                nc.vector.tensor_tensor(lo, wg_view(g), f32(hi), ALU.subtract).then_inc(wT_lo, 1)
            with dve.Fori(1, B - 1) as b:
                batch(b * TPB)
            batch(T - TPB, more=False)
            nc.vector.drain().then_inc(phase_a, 1)

            def x1(t):
                return resid[:, bass.ds(t, 1), :, :]

            def amax_x(n, s):
                after(dve, scale_s, n - 1)
                nc.vector.tensor_reduce(am[:, s, 0:DB], x1(n).rearrange("p t g e -> p (t g) e"), AX.X, ALU.max,
                                        apply_absolute_value=True).then_inc(am_s, 1 if there(n - LAG) else 2)

            def amax_h(n, s):
                after(dve, scale_s, n - 1)
                dve.wait_ge(h_s, 2 * n - (2 * LAG - 2))
                nc.vector.tensor_reduce(am[:, s, DB:VB], blocks(h[:, s, :]), AX.X, ALU.max,
                                        apply_absolute_value=True).then_inc(am_s, 1 if there(n) else 2)

            def joint_scales(n, s):
                a, b = (c // BLK for c in columns(n))
                dve.wait_ge(am_s, 2 * n + 2)
                after(dve, deq_s, n - 1)
                scales_of(am[:, s, a:b], sn[:, s, a:b], s14[:, s, a:b], inv[:, s, a:b], sn_s, scale_s, n + 1)

            def round_off(n, s):
                a, b = columns(n)
                dve.wait_ge(f16_s, n + 1)
                half_up(vq[:, s, :].bitcast(U16)[:, a:b], half_s, round_s, n + 1)

            def low(n, s):
                parts = bank_chunks(n)
                for i, (view, a, b) in enumerate(parts):
                    dve.wait_ge(vT_hi_s, 2 * n + 1 + i)
                    last = nc.vector.tensor_tensor(vT_lo[:, s, a:b, :], view, f32(vT_hi[:, s, a:b, :]), ALU.subtract)
                last.then_inc(vT_lo_s, 1)

            def gated(t, s, half):
                dve.wait_ge(g_act, 2 * t + (half + 1))
                if half == 0:
                    if there(t - 2):
                        dve.wait_ge(scaled, t + (LAG - 1))
                nc.vector.tensor_tensor(h[:, s, half * IH:(half + 1) * IH], gact[:, half, :],
                                        ps[2 * half + 1][:, 0:IH], ALU.mult).then_inc(h_s, 1)

            def residual(t, s):
                dve.wait_ge(dn_ps, t + 1)
                after(dve, ob_s, t - 1)
                nc.vector.tensor_tensor(r3[:, s, :].unsqueeze(1), ps[6 + s][:, 0:D].unsqueeze(1),
                                        x1(t).rearrange("p t g e -> p t (g e)"), ALU.add).then_inc(r3_s, 1)

            def ln3_stats(t, s):
                dve.wait_ge(r3_s, t + 1)
                nc.vector.bn_stats(st3[:, s, :], r3[:, s, :]).then_inc(st3_s, 1)

            def ln3_mean(t, s):
                dve.wait_ge(st3_s, t + 1)
                nc.vector.nop(nofuse=True)
                nc.vector.bn_aggr(mv3[:, s, :], st3[:, s, :]).then_inc(mv3_s, 1)

            def ln3_var(t, s):
                dve.wait_ge(mv3_s, t + 1)
                nc.vector.tensor_scalar(ve3[:, s:s + 1], mv3[:, s, 1:2], EPS_LN, None, ALU.add).then_inc(ve3_s, 1)

            def step(t, n):
                s, o = n % 2, (n + 1) % 2
                done = there(t - 5)
                if joint(t + 2):
                    round_off(t + 2, s)
                if done:
                    residual(t - 5, o)
                if there(t + 4):
                    amax_x(t + 4, s)
                if there(t):
                    gated(t, s, 0)
                if done:
                    ln3_stats(t - 5, o)
                if joint(t + 1):
                    low(t + 1, o)
                if done:
                    ln3_mean(t - 5, o)
                if there(t):
                    gated(t, s, 1)
                if done:
                    ln3_var(t - 5, o)
                if there(t):
                    amax_h(t + 4, s)
                if joint(t + 4):
                    joint_scales(t + 4, s)

            def begin(s):
                if s == 1:
                    dve.wait_ge(phase_a, 4)
                    nc.vector.memset(va[:, :, VW:VC * P], 0.0).then_inc(pad_s, 1)
                    dve.wait_ge(x1_s, 4)
                    amax_x(0, 0)
                    joint_scales(0, 0)
                elif s == 2:
                    amax_x(1, 1)
                    joint_scales(1, 1)
                    round_off(0, 0)
                elif s == 3:
                    amax_x(2, 0)
                    round_off(1, 1)
                    joint_scales(2, 0)
                    low(0, 0)
                elif s == 4:
                    amax_x(3, 1)
                    joint_scales(3, 1)

            batch(T, new=False, more=False)
            for t in range(12):
                step(t, t % 4)
                if t == 0:
                    ln2_variance(T - TPB, 3)
                elif t == 1:
                    ln2_shift(T - TPB, 3)
            dve.wait_ge(x1_s, T)
            with dve.Fori(3, T // 4 - 1) as i:
                for n in range(4):
                    step(i * 4 + n, n)
            for t in range(T - 4, T + 6):
                step(t, t % 4)

        @block.gpsimd
        def _(pool):
            nc.gpsimd.memset(ident[:, :], 0.0).then_inc(consts_set, 1)
            pool.wait_ge(consts_set, 1)
            nc.gpsimd.affine_select(out=ident[:, :], in_=ident[:, :], compare_op=ALU.not_equal, fill=1.0, base=0,
                                    pattern=[[-1, P]], channel_multiplier=1).then_inc(consts_set, 1)
            pool.wait_ge(consts_set, 2)
            nc.gpsimd.memset(headmask[:, :], 1.0).then_inc(mask_s, 1)
            hm = headmask[:, :].rearrange("p (g e) -> p g e", e=HD)
            pool.wait_ge(mask_s, 1)
            nc.gpsimd.affine_select(out=hm, in_=hm, compare_op=ALU.is_ge, fill=0.0, base=0,
                                    pattern=[[-HD, P // HD], [0, HD]], channel_multiplier=1).then_inc(mask_s, 1)
            pool.wait_ge(mask_s, 2)
            nc.gpsimd.affine_select(out=hm, in_=hm, compare_op=ALU.is_ge, fill=0.0, base=HD - 1,
                                    pattern=[[HD, P // HD], [0, HD]], channel_multiplier=-1).then_inc(consts_set, 2)
            pool.wait_ge(small_set, 4)
            pool.wait_ge(consts_in, 3 * 16)
            pool.wait_ge(rows_in, 4 * 16)

            def w_scaled_chunk(c):
                a, b = CH[c]
                pool.wait_ge(w_scale_s, c + 1)
                nc.gpsimd.tensor_tensor(blocks(wy[:, a:b]), blocks(wraw[:, a:b]), each(winv[:, a // BLK:b // BLK]),
                                        ALU.mult).then_inc(w_scaled, 1)

            def w_deq_chunk(c):
                a, b = CH[c]
                pool.wait_ge(w_rounded, c + 1)
                nc.gpsimd.tensor_tensor(blocks(wa[:, a:b]), blocks(wqn[:, a:b]), each(ws14[:, a // BLK:b // BLK]),
                                        ALU.mult).then_inc(w_deq, 1)

            def x_bias(t0, r):
                pool.wait_ge(x_in[r], t0 * 2 + 16)
                after(pool, w1_s, t0 - TPB + (2 * r + 2))
                nc.gpsimd.tensor_tensor(xbeta[:, 2 * r:2 * r + 2, :], xin[:, 2 * r:2 * r + 2, :],
                                        beta_b[:, :].unsqueeze(1).broadcast_to([P, 2, D]),
                                        ALU.add).then_inc(x_plus, 2)

            def k_normalise(t0, r):
                pool.wait_ge(k_norm, t0 + (2 * r + 2))
                after(pool, kv_acc, t0 + (2 * r - 2))
                nc.gpsimd.tensor_tensor(khat[:, r % 2, :, :].rearrange("p j (g e) -> p (j g) e", e=HD),
                                        blocks(kf[:, r % 2, :]), each(knorm[:, r % 2, :]),
                                        ALU.mult).then_inc(k_hat, 2)

            def ln1_affine(t0, r):
                v = t0 + (2 * r + 2)
                pool.wait_ge(z1_s, v)
                nc.gpsimd.tensor_tensor(z1, z1, gamma_b[:, :].unsqueeze(1).broadcast_to([P, 2, D]),
                                        ALU.mult).then_inc(zg_s, 2)
                pool.wait_ge(zg_s, v)
                nc.gpsimd.tensor_tensor(w1[:, r % 2, :, :], z1, xbeta[:, 2 * r:2 * r + 2, :], ALU.add).then_inc(w1_s, 2)

            def root(t0, r, ve, rstd, s_ve, s_rstd):
                pool.wait_ge(s_ve, t0 + (2 * r + 2))
                nc.gpsimd.tensor_tensor(rstd, ve, mhalf[:, :].broadcast_to([P, 2]), ALU.pow).then_inc(s_rstd, 2)

            def batch(t0, new=True, old=True, more=True, weights=False):
                u0 = t0 - TPB
                for s in range(STEPS):
                    if new and 3 <= s <= NP:
                        k_normalise(t0, s - 1)
                    if old and (s == NP or s > NP and new):
                        root(u0, s - 2, ve2[:, s % 2, :], rstd2[:, s % 2, :], ve2_s, rstd2_s)
                    if old and 0 <= s - 1 < NP:
                        ln1_affine(u0, s - 1)
                    if new and 0 < s < 3:
                        k_normalise(t0, s - 1)
                    if old and 2 <= s < NP:
                        root(u0, s - 2, ve2[:, s % 2, :], rstd2[:, s % 2, :], ve2_s, rstd2_s)
                    if old and s < NP:
                        root(u0, s, ve1, rstd1, ve1_s, rstd1_s)
                    if new and 0 <= s - 1 < NP:
                        x_bias(t0, s - 1)
                    if not new:
                        begin(s)
                    if weights and 0 <= s - 1 < len(CH):
                        w_scaled_chunk(s - 1)
                    if weights and 0 <= s - 3 < len(CH):
                        w_deq_chunk(s - 3)

            batch(0, old=False, weights=True)
            with pool.Fori(1, B - 1) as b:
                batch(b * TPB)
            batch(T - TPB, more=False)
            nc.gpsimd.drain().then_inc(phase_a, 1)

            def over_scales(n, s):
                pool.wait_ge(scale_s, n + 1)
                after(pool, f16_s, n - 1)
                if there(n - LAG):
                    last = nc.gpsimd.tensor_tensor(blocks(vy[:, s, D:VW]), blocks(h[:, s, :]), each(inv[:, s, DB:VB]),
                                                   ALU.mult)
                if there(n):
                    last = nc.gpsimd.tensor_tensor(blocks(vy[:, s, 0:D]),
                                                   resid[:, bass.ds(n, 1), :, :].rearrange("p t g e -> p (t g) e"),
                                                   each(inv[:, s, 0:DB]), ALU.mult)
                last.then_inc(scaled, 1)

            def dequantise(n, s):
                a, b = columns(n)
                pool.wait_ge(round_s, n + 1)
                after(pool, vT_ps, n - 1)
                nc.gpsimd.tensor_tensor(blocks(va[:, s, a:b]), blocks(vq[:, s, :].bitcast(F16)[:, a:b]),
                                        each(s14[:, s, a // BLK:b // BLK]), ALU.mult).then_inc(deq_s, 1)

            def ln3_root(t, s):
                pool.wait_ge(ve3_s, t + 1)
                nc.gpsimd.tensor_tensor(rstd3[:, s:s + 1], ve3[:, s:s + 1], mhalf[:, :], ALU.pow).then_inc(rstd3_s, 1)
                nc.gpsimd.tensor_tensor(nmean3[:, s:s + 1], mv3[:, s, 0:1], mone[:, :], ALU.mult).then_inc(nmean3_s, 1)
                pool.wait_ge(rstd3_s, t + 1)
                pool.wait_ge(nmean3_s, t + 1)
                nc.gpsimd.tensor_tensor(nmr3[:, s:s + 1], nmean3[:, s:s + 1], rstd3[:, s:s + 1],
                                        ALU.mult).then_inc(nmr3_s, 1)

            def step(t, n):
                if joint(t + 3):
                    over_scales(t + 3, (n + 1) % 2)
                if joint(t + 2):
                    dequantise(t + 2, n % 2)
                if there(t - 5):
                    ln3_root(t - 5, (n + 1) % 2)

            def begin(s):
                if s == 1:
                    pool.wait_ge(phase_a, 4)
                    over_scales(0, 0)
                elif s == 2:
                    over_scales(1, 1)
                    dequantise(0, 0)
                elif s == 3:
                    dequantise(1, 1)
                    over_scales(2, 0)

            batch(T, new=False, more=False)
            for t in range(12):
                step(t, t % 4)
                if t == 0:
                    root(T - TPB, 3, ve2[:, 1, :], rstd2[:, 1, :], ve2_s, rstd2_s)
            with pool.Fori(3, T // 4 - 1) as i:
                for n in range(4):
                    step(i * 4 + n, n)
            for t in range(T - 4, T + 6):
                step(t, t % 4)


_INS = ["L0_attn_x", "L0_attn_Wq", "L0_attn_bq", "L0_attn_Wk", "L0_attn_bk", "L0_attn_Wv", "L0_attn_bv", "L0_attn_Wo",
        "L0_attn_bo", "L0_attn_gamma", "L0_attn_beta", "L0_ffn_w_gate", "L0_ffn_w_up", "L0_ffn_w_down"]


def kernel(**inputs):
    import numpy as _np
    import concourse.bacc as _bacc
    from concourse import mybir as _mybir
    from concourse.bass_utils import run_bass_kernel_spmd as _run

    nc = _bacc.Bacc("TRN2", target_bir_lowering=False, num_devices=1)
    arrays, args = {}, []
    for name in _INS:
        a = _np.ascontiguousarray(inputs[name])
        arrays[f"in_{name}_dram"] = a
        args.append(nc.dram_tensor(f"in_{name}_dram", a.shape, _mybir.dt.from_np(a.dtype), kind="ExternalInput").ap())
    shape = inputs["L0_attn_x"].shape
    args.append(nc.dram_tensor("out_dram", shape, _mybir.dt.float32, kind="ExternalOutput").ap())
    build(nc, *args)
    r = _run(nc, [arrays], core_ids=[0])
    return r.results[0]["out_dram"]
```
